# Optimizing a Trainium2 kernel written in Bass

```python
import numpy as np
import jax
import jax.numpy as jnp

def _softmax(x, axis=-1):
    return jax.nn.softmax(x, axis=axis)

def _gelu(x):
    return jax.nn.gelu(x, approximate=True)

def _silu(x):
    return jax.nn.silu(x)

def _sigmoid(x):
    return jax.nn.sigmoid(x)

def _layernorm(x, axis=-1, eps=1e-05):
    m = jnp.mean(x, axis=axis, keepdims=True)
    v = jnp.var(x, axis=axis, keepdims=True)
    return (x - m) / jnp.sqrt(v + eps)

def _scatter_add(tgt, idx, src, axis=0):
    return tgt.at[idx].add(src)

def _segment_sum(src, seg, n):
    return jax.ops.segment_sum(src, seg, n)
kernel_name = 'mk_gnn_ffn_d1_gnn_r8_0b0455'

def setup_inputs(seed: int=0):
    np.random.seed(seed)
    _w = jnp.asarray

    def _rec_inputs():
        import jax
        import jax.numpy as jnp
        _gk = jax.random.key(seed)
        x = -0.0001394 + 0.9999 * jax.random.normal(jax.random.fold_in(_gk, 1), (1250, 768), jnp.float32)
        src = jax.random.randint(jax.random.fold_in(_gk, 2), (20000,), 0, 1250, jnp.int32)
        dst = jnp.minimum((1250 * jax.random.uniform(jax.random.fold_in(_gk, 3), (20000,)) ** 2.0).astype(jnp.int32), 9999)
        _o = jnp.argsort(dst, stable=True)
        src = src[_o]
        dst = dst[_o]
        return (x, src, dst)
    x, src, dst = _rec_inputs()

    def _L0_gnn_setup():
        import jax, jax.numpy as jnp
        import numpy as np
        N = 6250
        E = 31250
        H = 12
        D = 64
        NEG_SLOPE = 0.2
        key = jax.random.key(seed)
        k1, k2, k3, k4, k5, k6, k7 = jax.random.split(key, 7)
        h = jax.random.normal(k1, (N, H * D), dtype=jnp.float32)
        src = jnp.concatenate([jnp.arange(N, dtype=jnp.int32), jax.random.randint(k2, (E - N,), 0, N, dtype=jnp.int32)])
        dst = jnp.concatenate([jnp.arange(N, dtype=jnp.int32), jax.random.randint(k3, (E - N,), 0, N, dtype=jnp.int32)])
        xav = 1.414 / np.sqrt(D)
        W_fc = jax.random.normal(k4, (D, D), dtype=jnp.float32) * xav
        attn_l = jax.random.normal(k5, (H, D), dtype=jnp.float32) * 0.15
        attn_r = jax.random.normal(k6, (H, D), dtype=jnp.float32) * 0.15
        W_res = jax.random.normal(k7, (D, D), dtype=jnp.float32) * xav
        return {'h': h, 'W_fc': W_fc, 'attn_l': attn_l, 'attn_r': attn_r, 'W_res': W_res, 'src': src, 'dst': dst}
    _L0_gnn_all = _L0_gnn_setup()
    _L0_gnn_in = {k: v for k, v in _L0_gnn_all.items() if k in ('W_fc', 'attn_l', 'attn_r', 'W_res')}
    del _L0_gnn_all

    def _L0_ffn_setup():
        import jax, jax.numpy as jnp
        import numpy as np
        E, TOPK = (32, 2)
        D, HID, BOT, OUT = (768, 256, 256, 768)
        B, S = (2, 128)
        key = jax.random.key(seed)
        ks = jax.random.split(key, 7)
        p = lambda k, shape: jax.random.normal(k, shape, dtype=jnp.float32) * 0.02
        return {'x': jax.random.normal(ks[0], (B, S, D), dtype=jnp.float32), 'gate_w': p(ks[1], (E, D)), 'W1': p(ks[2], (E, D, HID)), 'b1': jnp.zeros((E, HID), jnp.float32), 'W2': p(ks[3], (E, HID, HID)), 'b2': jnp.zeros((E, HID), jnp.float32), 'W3': p(ks[4], (E, HID, BOT)), 'b3': jnp.zeros((E, BOT), jnp.float32), 'Wl': p(ks[5], (E, BOT, OUT)), 'bl': jnp.zeros((E, OUT), jnp.float32)}
    _L0_ffn_all = _L0_ffn_setup()
    _L0_ffn_in = {k: v for k, v in _L0_ffn_all.items() if k in ('gate_w', 'W1', 'b1', 'W2', 'b2', 'W3', 'b3', 'Wl', 'bl')}
    del _L0_ffn_all
    return {'x': x, 'src': src, 'dst': dst, 'L0_gnn_W_fc': _L0_gnn_in['W_fc'], 'L0_gnn_attn_l': _L0_gnn_in['attn_l'], 'L0_gnn_attn_r': _L0_gnn_in['attn_r'], 'L0_gnn_W_res': _L0_gnn_in['W_res'], 'L0_ffn_gate_w': _L0_ffn_in['gate_w'], 'L0_ffn_W1': _L0_ffn_in['W1'], 'L0_ffn_b1': _L0_ffn_in['b1'], 'L0_ffn_W2': _L0_ffn_in['W2'], 'L0_ffn_b2': _L0_ffn_in['b2'], 'L0_ffn_W3': _L0_ffn_in['W3'], 'L0_ffn_b3': _L0_ffn_in['b3'], 'L0_ffn_Wl': _L0_ffn_in['Wl'], 'L0_ffn_bl': _L0_ffn_in['bl']}

def reference(x, src, dst, L0_gnn_W_fc, L0_gnn_attn_l, L0_gnn_attn_r, L0_gnn_W_res, L0_ffn_gate_w, L0_ffn_W1, L0_ffn_b1, L0_ffn_W2, L0_ffn_b2, L0_ffn_W3, L0_ffn_b3, L0_ffn_Wl, L0_ffn_bl):
    import jax
    import jax.numpy as jnp

    def _L0_gnn_ref(h, W_fc, attn_l, attn_r, W_res, src, dst):
        import jax, jax.numpy as jnp
        import numpy as np
        N = 6250
        E = 31250
        H = 12
        D = 64
        NEG_SLOPE = 0.2
        n = h.shape[0]
        hh = h.reshape(n, H, D)
        ft = jnp.einsum('nhd,ed->nhe', hh, W_fc)
        a1 = jnp.einsum('nhd,hd->nh', ft, attn_l)
        a2 = jnp.einsum('nhd,hd->nh', ft, attn_r)
        e = jax.nn.leaky_relu(a1[src] + a2[dst], negative_slope=NEG_SLOPE)
        m = jax.ops.segment_max(e, dst, num_segments=n)
        ee = jnp.exp(e - m[dst])
        denom = jax.ops.segment_sum(ee, dst, num_segments=n)
        alpha = ee / denom[dst]
        agg = jax.ops.segment_sum(alpha[:, :, None] * ft[src], dst, num_segments=n)
        res = jnp.einsum('nhd,ed->nhe', hh, W_res)
        return jax.nn.relu((res + agg).reshape(n, H * D))

    def _L0_ffn_ref(x, gate_w, W1, b1, W2, b2, W3, b3, Wl, bl):
        import jax, jax.numpy as jnp
        import numpy as np
        E, TOPK = (32, 2)
        D, HID, BOT, OUT = (768, 256, 256, 768)
        B, S = (2, 128)
        Bz, Sl, d = x.shape
        xt = x.reshape(-1, d)
        scores = jax.nn.softmax(xt @ gate_w.T, axis=-1)
        topk_w, topk_idx = jax.lax.top_k(scores, TOPK)
        topk_w = topk_w / (topk_w.sum(-1, keepdims=True) + 1e-20)
        gelu = lambda v: jax.nn.gelu(v, approximate=False)
        h = gelu(jnp.einsum('nd,edh->enh', xt, W1) + b1[:, None, :])
        h = gelu(jnp.einsum('enh,ehg->eng', h, W2) + b2[:, None, :])
        z = jnp.einsum('eng,egb->enb', h, W3) + b3[:, None, :]
        out_all = jnp.einsum('enb,ebo->eno', z, Wl) + bl[:, None, :]
        sel = jnp.take_along_axis(out_all.transpose(1, 0, 2), topk_idx[:, :, None], axis=1)
        y = (sel * topk_w[:, :, None]).sum(axis=1)
        return y.reshape(Bz, Sl, OUT)
    x = x + _L0_gnn_ref(_layernorm(x, axis=-1), L0_gnn_W_fc, L0_gnn_attn_l, L0_gnn_attn_r, L0_gnn_W_res, src, dst)
    x = x + _L0_ffn_ref(_layernorm(x, axis=-1)[None], L0_ffn_gate_w, L0_ffn_W1, L0_ffn_b1, L0_ffn_W2, L0_ffn_b2, L0_ffn_W3, L0_ffn_b3, L0_ffn_Wl, L0_ffn_bl)[0]
    return x

_drawn_inputs = setup_inputs


def setup_inputs(seed=0):
    import zlib

    import numpy as np

    out = dict(_drawn_inputs(seed))
    spreads = {'L0_ffn_b1': (0.0, 0.8),
     'L0_ffn_b2': (0.0, 0.8),
     'L0_ffn_b3': (0.0, 0.509),
     'L0_ffn_bl': (0.0, 0.8)}
    factors = {'L0_ffn_W1': 8.0, 'L0_ffn_W2': 8.0, 'L0_ffn_W3': 8.0, 'L0_ffn_Wl': 3.492}
    for name, (base, spread) in spreads.items():
        noise = np.random.default_rng([zlib.crc32(name.encode()), seed]).standard_normal(out[name].shape)
        drawn = base * np.exp(spread * noise) if base else spread * noise
        out[name] = jnp.asarray(drawn.astype(out[name].dtype))
    for name, factor in factors.items():
        out[name] = (out[name] * factor).astype(out[name].dtype)
    return out
```

```python
from contextlib import ExitStack

import concourse.bass as bass
from concourse import mybir

ALU = mybir.AluOpType
ACT = mybir.ActivationFunctionType
AX = mybir.AxisListType
F32 = mybir.dt.float32
BF16 = mybir.dt.bfloat16
F16 = mybir.dt.float16
I32 = mybir.dt.int32
U32 = mybir.dt.uint32
RMAX = bass.bass_isa.ReduceOp.max

P = 128
SLOPE = 0.2
LN_EPS = 1e-5
GSIZE = 2
WIN = 48
CRING = 8
WSTEP = CRING // GSIZE
WRING = 2
SRING = 4
NEG = 4
WSLOTS = 4
MAX_RANGE = 80.0
MAX_COUNT = 256.0
FAR = 8192.0


class Chain:

    def __init__(self, eng, sem):
        self.eng, self.sem, self.n = eng, sem, 0

    def link(self, ins):
        ins.then_inc(self.sem, 1)
        self.n = self.n + 1
        self.eng.wait_ge(self.sem, self.n)


def at_col(a, i):
    return a[:, i:i + 1] if isinstance(i, int) else a[:, bass.ds(i, 1)]


def at_mid(a, i):
    return a[:, i] if isinstance(i, int) else a[:, bass.ds(i, 1)].squeeze(1)


def run(eng, n, body, chain=None, links=0, first=False):
    n0 = chain.n if chain else 0
    if first:
        body(0, False)
    with eng.Fori(int(first), n - 1) as q:
        if chain:
            chain.n = n0 + q * links
        body(q, False)
    if chain:
        chain.n = n0 + (n - 1) * links
    body(n - 1, True)


def gnn_moe_kernel(nc, x, src, dst, W_fc, attn_l, attn_r, W_res, gate_w,
                   W1, b1, W2, b2, W3, b3, Wl, bl, out, h2_dram, y_dram, res_dram):
    N, F = x.shape
    H, D = attn_l.shape
    E = src.shape[0]
    NX, _, HID = W1.shape
    NT = -(-N // P)
    NP = NT * P
    LAST = N - (NT - 1) * P
    C6 = F // P
    HC = HID // P
    ET = E // P
    EREM = E - ET * P
    ETP = 160
    ET1 = ETP - P
    NG = ETP // GSIZE
    CW = NP + WIN
    KW = NT * WIN
    D1 = D + 1
    ITS = [(0, NT // 2), (NT // 2, NT)]
    PART = NT // 2 * P
    MORE = -(-N // WIN)
    OT = 2 * N // P
    assert NT == 10 and F == 768 and H == 12 and D == 64 and NX == 32 and HID == 256

    with ExitStack() as ctx:
        def sb(name, shape, dt=F32):
            return ctx.enter_context(nc.sbuf_tensor(name, shape, dt))

        def sem(name):
            return ctx.enter_context(nc.semaphore(name))

        banks = [ctx.enter_context(nc.psum_tensor(f"bank{i}", [P, 512], F32)) for i in range(6)]
        duo = ctx.enter_context(nc.psum_tensor("duo", [P, 2, 512], F32))

        ft = sb("ft", [P, NT * H * D1])
        xp_mem = sb("xp_mem", [P, 2 * 1950 + 1300])
        c_mem = sb("c_mem", [P, NT * CW])
        cbf_mem = sb("cbf_mem", [P, NT * NP // 2])
        agg = sb("agg", [P, NT * H * D1])
        w_mem = sb("w_mem", [P, 16 * HID])

        ft4 = ft[:, :].rearrange("p (t h e) -> p t h e", t=NT, h=H)
        agg4 = agg[:, :].rearrange("p (t h e) -> p t h e", t=NT, h=H)
        xt = [agg[:, F * i:F * (i + 1)] for i in range(2)]
        ht = [agg[:, F * (2 + i):F * (3 + i)] for i in range(2)]
        hTt = [agg[:, F * (4 + i):F * (5 + i)].rearrange("p (c n) -> p c n", c=C6) for i in range(2)]
        rt = [agg[:, F * (6 + i):F * (7 + i)] for i in range(2)]
        c32 = c_mem[:, :].rearrange("p (t w) -> p t w", t=NT)
        cbf = cbf_mem[:, :].bitcast(BF16).rearrange("p (t n) -> p t n", t=NT)
        oha = xp_mem[:, 0:CRING * P // 2].bitcast(BF16).rearrange("p (r n) -> p r n", r=CRING)
        ohb = xp_mem[:, CRING * P // 2:CRING * P // 2 + CRING * KW // 2].bitcast(BF16)\
            .rearrange("p (r n) -> p r n", r=CRING)
        xp = [xp_mem[:, 1950 * i:1950 * (i + 1)].bitcast(BF16)
              .rearrange("p (t k b e) -> p t k b e", t=NT, k=3, b=2) for i in range(2)]
        x12 = xp_mem[:, 3900:5200].rearrange("p (t b e) -> p t b e", t=NT, b=2)
        cm = c_mem[:, 0:2 * NT * NP // 2].bitcast(BF16)
        mask, nmask = [], []
        off = 0
        for lo, hi in ITS:
            n = NT * (hi - lo) * P
            mask.append(cm[:, off:off + n].rearrange("p (t n) -> p t n", t=NT))
            nmask.append(cm[:, off + n:off + 2 * n].rearrange("p (t n) -> p t n", t=NT))
            off += 2 * n
        base = c_mem[:, 0:NT * F].rearrange("p (t f) -> p t f", t=NT)
        wslot = [w_mem[:, :], cbf_mem[:, 0:16 * HID], xp_mem[:, 0:16 * HID],
                 c_mem[:, NT * F:NT * F + 16 * HID]]
        w1s = [w[:, 0:C6 * HID].rearrange("p (c m) -> p c m", c=C6) for w in wslot]
        w2s = [w[:, 6 * HID:8 * HID].rearrange("p (c m) -> p c m", c=HC) for w in wslot]
        w3s = [w[:, 8 * HID:10 * HID].rearrange("p (c m) -> p c m", c=HC) for w in wslot]
        wls = [w[:, 10 * HID:16 * HID].rearrange("p (c m) -> p c m", c=HC) for w in wslot]
        xg = [ft[:, F * i:F * (i + 1)] for i in range(2)]
        xgT = [ft[:, F * (2 + i):F * (3 + i)].rearrange("p (c n) -> p c n", c=C6) for i in range(2)]
        ys = [ft[:, F * (4 + i):F * (5 + i)] for i in range(2)]
        hid = [[ft[:, F * 6 + HID * (3 * i + k):F * 6 + HID * (3 * i + k + 1)]
                .rearrange("p (c n) -> p c n", c=HC) for i in range(2)] for k in range(3)]
        YR = 4
        ypair = [agg[:, 2 * F * i:2 * F * (i + 1)] for i in range(YR)]
        xres = [[xp_mem[:, F * (2 * k + i):F * (2 * k + i + 1)] for i in range(2)] for k in range(2)]

        def carve(mem, at_float, shape, dt=F32, parts=P):
            n = 1
            for d in shape:
                n *= d
            a = mem[0:parts, at_float:at_float + n]
            if dt != F32:
                a = a.bitcast(dt)
            if len(shape) > 1:
                names = "abcd"[:len(shape)]
                a = a.rearrange(f"p ({' '.join(names)}) -> p {' '.join(names)}",
                                **{c: d for c, d in zip(names[:-1], shape)})
            return a

        o = CRING * (P + KW) // 2
        edges = carve(xp_mem, o, [4, P], I32)
        edges_f = carve(xp_mem, o + 4 * P, [4, P])
        sd_t = carve(xp_mem, o + 8 * P, [2, ETP])
        o += 8 * P + 2 * ETP
        si, jt_i, jp_i = [carve(xp_mem, o + ETP * i, [ETP], I32) for i in range(3)]
        jt_f, dd, pen = [carve(xp_mem, o + ETP * i, [ETP]) for i in range(3, 6)]
        o = 8 * F
        bdn = carve(agg, o, [2, P])
        bd = carve(agg, o + 2 * P, [2, P])
        at = carve(agg, o + 4 * P, [C6, 2 * H])
        bda = carve(agg, o + 4 * P + C6 * 2 * H, [C6, 2 * H])
        pen2 = carve(xp_mem, CRING * (P + KW) // 2 + 4 * P, [ETP])
        gate_n = carve(w_mem, 0, [F], parts=NX)
        bn = carve(w_mem, F, [3, HID], parts=NX)
        o = 16 * HID
        mk = carve(cbf_mem, o, [NT, 2, NX])
        o += NT * 2 * NX
        lg, ex, rk, gm = [carve(cbf_mem, o + NT * NX * i, [NT, NX]) for i in range(4)]
        sla = carve(xp_mem, 16 * HID, [4, P])
        o = 16 * HID + 4 * P
        msum, macc = [carve(xp_mem, o + NT * NX // 2 * i, [NT * NX // 2])
                      .bitcast(BF16).rearrange("p (t n) -> p t n", t=NT) for i in range(2)]
        slb = carve(ft, 8 * F, [NT, 2, 2, NX])
        rkm = carve(ft, 8 * F + NT * 4 * NX, [NT, NX])

        c_in = cbf_mem[:, 3 * NP:4 * NP].rearrange("p (t n) -> p t n", t=NT)
        c_row, none_row, e_row, p_row = [cbf_mem[:, i * NP:(i + 1) * NP] for i in range(4)]
        p_t = cbf_mem[:, 4 * NP:5 * NP].rearrange("p (t n) -> p t n", t=NT)
        o = 2 * F
        ov_a = carve(agg, 0, [P])
        ov_b = carve(agg, P, [2, OT])
        ov_v = carve(agg, 2 * P, [2, OT])
        ov_f = carve(agg, 3 * P, [OT])
        ov_s, ov_g = [carve(agg, 3 * P + 32 * i, [OT], I32) for i in (1, 2)]
        ov_rank_i, ov_hi_i, ov_lo_i = [carve(agg, 4 * P + 128 + 32 * i, [NT, 2], I32) for i in range(3)]
        ov_hi, ov_lo, ov_ge, ov_base = [carve(agg, 4 * P + 224 + 32 * i, [NT, 2]) for i in range(4)]
        ov_n, ov_first, ov_end = [carve(agg, 7 * P + 32 * i, [NX]) for i in range(3)]
        ov_ni = carve(agg, 7 * P + 96, [NX], I32)
        ov_tab = carve(agg, 8 * P, [OT, NX])
        ov_tab2 = carve(agg, 8 * P + OT * NX, [OT, NX])
        ov_ex = carve(agg, 8 * P + 2 * OT * NX, [OT])
        ov_exi = carve(agg, 8 * P + 2 * OT * NX + 32, [OT], I32)
        ov_m = carve(agg, 8 * P + 2 * OT * NX + 64, [NT, NX])
        iota_o = carve(agg, 8 * P + 2 * OT * NX + 64 + NT * NX, [OT])

        ident = sb("ident", [P, P])
        ones_f = sb("ones_f", [P, P])
        ones_b = sb("ones_b", [P, P], BF16)
        before = sb("before", [P, P], BF16)
        iota_p = sb("iota_p", [P, P], F16)
        iota_k = sb("iota_k", [P, KW], F16)
        iota_x = sb("iota_x", [P, NX])
        pair_id = sb("pair_id", [P, NT * 2])
        valid = sb("valid", [P, 1])
        tmin = sb("tmin", [P, 2])
        lo_row = sb("lo_row", [1, ETP])
        lo_min = sb("lo_min", [1, NG])
        lo_int = sb("lo_int", [1, NG], I32)
        key = sb("key", [P, ETP])
        jp_h = sb("jp_h", [P, ETP], F16)
        bns = sb("bns", [P, 2, 6])
        mv = sb("mv", [P, 2])
        ve = sb("ve", [P, 1])
        sd = sb("sd", [P, 1])
        rstd = sb("rstd", [P, 1])
        a12 = sb("a12", [P, NT, 2 * H])
        na1 = sb("na1", [P, NT, H])
        far = sb("far", [P, 1])
        far_all = sb("far_all", [P, 1])
        red = sb("red", [P, 3])
        allr = sb("allr", [P, 3])
        flag_f = sb("flag_f", [1, 4])
        flags = sb("flags", [1, 3], I32)
        rank_max = sb("rank_max", [P, 1])
        rank_all = sb("rank_all", [P, 1])
        m_row = sb("m_row", [P, 1])
        n_all = sb("n_all", [P, NX])
        nA = sb("nA", [P, 2])
        sA = sb("sA", [P, NT, H])
        fa = sb("fa", [P, 2, NT, H])
        e12 = sb("e12", [P, 2, NT, H])
        f12 = sb("f12", [P, 2, NT, H])
        a2T = sb("a2T", [H, NP])
        a2m = sb("a2m", [H, NP])
        a2b = sb("a2b", [P, NP])
        gmT = a2b[0:NX, :]
        t2 = sb("t2", [P, SRING, D1])
        rden = sb("rden", [P, NT, H])
        gateT = sb("gateT", [P, C6, NX])
        bT = sb("bT", [P, 3, HC, NX])
        bln = sb("bln", [NX, F])
        mx8 = sb("mx8", [P, NT, 8])
        ix8 = sb("ix8", [P, NT, 8], U32)
        ixf = sb("ixf", [P, NT, 2])
        ex1 = sb("ex1", [P, NT])
        pr = sb("pr", [P, 2, NT])
        psum_pr = sb("psum_pr", [P, NT])
        wk = sb("wk", [P, NT, 2])
        rank = sb("rank", [P, NT, 2])
        slot_v = sb("slot_v", [P, 2, NX])
        slot_f = sb("slot_f", [P, NX])
        slot_s = sb("slot_s", [P, NX], I32)
        slot_g = sb("slot_g", [P, NX], I32)
        gi = [sb(f"gi{i}", [P, 1], I32) for i in range(2)]
        so = [sb(f"so{i}", [P, 1], I32) for i in range(2)]

        (const_ready, pool_chain, dve_chain, edges_zeroed, edges_in, gnnw_zeroed, gnnw_in, small_in,
         edges_float, edges_turned, lo_ready, lo_spread, key_ready, oha_ready, ohb_ready, window_done,
         window_added, counts_ready, bd_turned, bd_ready, bda_done, bda_ready, var1_ready, sd1_ready, var2_ready, sd2_ready, h_ready, h_turned, hT_ready,
         ft_done, ft_ready, res_copied, red_ready, allr_ready, fa_ready, e_made, e_ready, a2_turned, a2T_ready,
         small_turned, smallT_ready, a2m_ready, a2_spread, a2b_ready, compared, mask_ready, x_made, hi_ready,
         rest_made, mid_ready, xp_ready, sums_done, t2_ready, sums_added, x1_ready, h2_ready, h2_turned,
         h2T_ready, logits_done, logits_read, ex_in, ex_lg, ex_made, ex_ready, m_ready, rank_done, gm_ready, gm_turned,
         gmT_ready, sl_ready, slots_done, slots_ready, bias_done, base_ready, xg_zeroed, xg_turned, xgT_a,
         xgT_d, l1_done, g1_ready, l2_done, g2_ready, l3_done, z_ready, l4a_done, l4_done, ya_ready,
         yd_ready, gathers_begun, scatters_begun, neg_ready, counts_zeroed, const2_ready, far_ready, far_all_ready, flag1_ready, more_step, flag2_ready, wide_step, attention_done, rank_max_ready, rank_all_ready, flag3_ready, extra_step, ex_in_w, ex_in_x, ex_out,
         sum_ready, out_done) = [sem(n) for n in (
             "const_ready pool_chain dve_chain edges_zeroed edges_in gnnw_zeroed gnnw_in small_in "
             "edges_float edges_turned lo_ready lo_spread key_ready oha_ready ohb_ready window_done "
             "window_added counts_ready bd_turned bd_ready bda_done bda_ready var1_ready sd1_ready var2_ready sd2_ready h_ready h_turned hT_ready "
             "ft_done ft_ready res_copied red_ready allr_ready fa_ready e_made e_ready a2_turned a2T_ready "
             "small_turned smallT_ready a2m_ready a2_spread a2b_ready compared mask_ready x_made hi_ready "
             "rest_made mid_ready xp_ready sums_done t2_ready sums_added x1_ready h2_ready h2_turned "
             "h2T_ready logits_done logits_read ex_in ex_lg ex_made ex_ready m_ready rank_done gm_ready gm_turned "
             "gmT_ready sl_ready slots_done slots_ready bias_done base_ready xg_zeroed xg_turned xgT_a "
             "xgT_d l1_done g1_ready l2_done g2_ready l3_done z_ready l4a_done l4_done ya_ready "
             "yd_ready gathers_begun scatters_begun neg_ready counts_zeroed const2_ready far_ready far_all_ready flag1_ready more_step flag2_ready wide_step attention_done rank_max_ready rank_all_ready flag3_ready extra_step ex_in_w ex_in_x ex_out "
             "sum_ready out_done").split()]
        x_in = [sem(f"x_in{i}") for i in range(2)]
        res_out = [sem(f"res_out{i}") for i in range(2)]
        xr_in = [sem(f"xr_in{i}") for i in range(2)]
        h2_out = [sem(f"h2_out{i}") for i in range(2)]
        w_in = [sem(f"w_in{i}") for i in range(WSLOTS)]
        xg_in = [sem(f"xg_in{i}") for i in range(2)]
        y_out = [sem(f"y_out{i}") for i in range(2)]
        ypair_in = [sem(f"ypair_in{i}") for i in range(YR)]

        MK = 8 + 5 * NG
        WH = 17
        W0, WT = 4, 6 + WH * H
        XS = 58
        X0, XK = XS + 4 * 2 * NT + 5, 20

        block = ctx.enter_context(nc.Block())

        def rows(t):
            return LAST if t == NT - 1 else P

        def chunks(a, c):
            n = a.shape[-1] // P
            return a.rearrange("p (q c) -> p c q", c=n)[:, c, :]


        @block.sync
        def _(sp):
            sp.wait_ge(edges_zeroed, 2)
            for k, a in enumerate((src, dst)):
                sp.dma_start(edges[:, k, :], a[0:P * P].rearrange("(t e) -> t e", e=P)).then_inc(edges_in, 16)
                sp.dma_start(edges[0:ET - P, 2 + k, :],
                             a[P * P:ET * P].rearrange("(t e) -> t e", e=P)).then_inc(edges_in, 16)
                sp.dma_start(edges[ET - P:ET - P + 1, 2 + k, 0:EREM],
                             a[ET * P:E].rearrange("(t e) -> t e", t=1)).then_inc(edges_in, 16)
            for t in range(2):
                sp.dma_start(xt[t], x[t * P:(t + 1) * P, :]).then_inc(x_in[t], 16)
            sp.wait_ge(gnnw_zeroed, 2)
            for k, a in enumerate((W_fc, W_res)):
                for b in range(2):
                    sp.dma_start(bdn[D * b:D * b + D, k, D * b:D * b + D], a).then_inc(gnnw_in, 16)
            with nc.allow_non_contiguous_dma(reason="attention vectors as columns"):
                for k, a in enumerate((attn_l, attn_r)):
                    for h in range(H):
                        c, b = h // 2, h % 2
                        sp.dma_start(at[D * b:D * b + D, c, k * H + h:k * H + h + 1],
                                     a[h:h + 1, :].rearrange("h e -> e h")).then_inc(gnnw_in, 16)
            sp.dma_start(gate_n[:, :], gate_w).then_inc(small_in, 16)
            for k, a in enumerate((b1, b2, b3)):
                sp.dma_start(bn[:, k, :], a).then_inc(small_in, 16)
            sp.dma_start(bln[:, :], bl).then_inc(small_in, 16)
            for t in range(2, NT + 2):
                if t < NT:
                    sp.wait_ge(h_ready, t - 1)
                    sp.dma_start(xt[t % 2][0:rows(t), :], x[t * P:t * P + rows(t), :]).then_inc(x_in[t % 2], 16)
                sp.wait_ge(res_copied, 3 * (t - 1))
                sp.dma_start(res_dram[(t - 2) * P:(t - 1) * P, :], rt[t % 2]).then_inc(res_out[t % 2], 16)

            def load_expert(e, s):
                for tile, w in ((w1s, W1), (w2s, W2), (w3s, W3), (wls, Wl)):
                    w_e = w[e] if isinstance(e, int) else w[bass.ds(e, 1), :, :].squeeze(0)
                    sp.dma_start(tile[s].rearrange("p c m -> p (c m)"),
                                 w_e.rearrange("(p c) m -> p (c m)", p=P)).then_inc(w_in[s], 16)

            sp.wait_ge(smallT_ready, 2)
            load_expert(0, 0)
            sp.wait_ge(attention_done, 1)
            for i in range(2):
                sp.wait_ge(res_out[i], 16 * (NT // 2))
            for t in range(NT):
                if t >= 2:
                    sp.wait_ge(x1_ready, t - 1)
                sp.dma_start(xres[0][t % 2][0:rows(t), :], x[t * P:t * P + rows(t), :]).then_inc(xr_in[t % 2], 16)
                sp.dma_start(xres[1][t % 2], res_dram[t * P:(t + 1) * P, :]).then_inc(xr_in[t % 2], 16)
                if t == 2:
                    load_expert(1, 1)
                if t == 4:
                    load_expert(3, 3)
                if t >= 1:
                    sp.wait_ge(h2_ready, t)
                    sp.dma_start(h2_dram[(t - 1) * P:t * P, :], xg[(t - 1) % 2]).then_inc(h2_out[(t - 1) % 2], 16)
            sp.wait_ge(h2_ready, NT)
            sp.dma_start(h2_dram[(NT - 1) * P:NT * P, :], xg[1]).then_inc(h2_out[1], 16)
            sp.wait_ge(x1_ready, NT)
            load_expert(2, 2)
            with sp.Fori(1, NX // WSLOTS) as q:
                for s in range(WSLOTS):
                    sp.wait_ge(l4_done, q * WSLOTS + (s + 1 - WSLOTS))
                    load_expert(q * WSLOTS + s, s)
            sp.wait_ge(flag3_ready, 1)
            with sp.If(sp.value_load(flags[0:1, 2:3]) > 0):
                with sp.Fori(0, OT) as j:
                    sp.wait_ge(extra_step, j * XK + (X0 + 1))
                    e = sp.snap(sp.value_load(at_col(ov_exi[0:1, :], j)), min_val=0, max_val=NX - 1)
                    for tile, w in ((w1s, W1), (w2s, W2), (w3s, W3), (wls, Wl)):
                        sp.dma_start(tile[0].rearrange("p c m -> p (c m)"),
                                     w[bass.ds(e, 1), :, :].squeeze(0)
                                     .rearrange("(p c) m -> p (c m)", p=P)).then_inc(ex_in_w, 16)
                sp.wait_ge(extra_step, X0 + OT * XK + 1)
            for i in range(2):
                sp.wait_ge(y_out[i], 16 * (NX // 2))
            for t in range(NT + YR - 1):
                if t < NT:
                    if t >= YR:
                        sp.wait_ge(sum_ready, t - YR + 1)
                    sp.dma_start(ypair[t % YR][0:rows(t), :],
                                 y_dram[2 * t * P:2 * (t * P + rows(t)), :]
                                 .rearrange("(p k) f -> p (k f)", k=2)).then_inc(ypair_in[t % YR], 16)
                u = t - (YR - 1)
                if u >= 0:
                    sp.wait_ge(sum_ready, u + 1)
                    sp.dma_start(out[u * P:u * P + rows(u), :], base[0:rows(u), u, :]).then_inc(out_done, 16)
            sp.wait_ge(out_done, 16 * NT)

        @block.gpsimd
        def _(pool):
            g = nc.gpsimd
            ch = Chain(pool, pool_chain)
            pool.sem_inc(xp_ready, 1)
            g.memset(edges[:, 2, :], 16000).then_inc(edges_zeroed, 1)
            g.memset(edges[:, 3, :], N - 1).then_inc(edges_zeroed, 1)
            g.memset(bdn[:, :, :], 0.0).then_inc(gnnw_zeroed, 1)
            g.memset(at[:, :, :], 0.0).then_inc(gnnw_zeroed, 1)
            ch.link(g.memset(ident[:, :], 0.0))
            ch.link(g.affine_select(out=ident[:, :], in_=ident[:, :], compare_op=ALU.not_equal, fill=1.0,
                                    base=0, pattern=[[-1, P]], channel_multiplier=1))
            ch.link(g.memset(ones_f[:, :], 1.0))
            for tile, pat in ((iota_p, [[1, P]]), (iota_k, [[1, KW]])):
                ch.link(g.iota(tile[:, :], pattern=pat, base=0, channel_multiplier=0,
                               allow_small_or_imprecise_dtypes=True))
            pool.sem_inc(const_ready, 1)
            g.memset(c_mem[:, :], 0.0).then_inc(counts_zeroed, 1)
            ch.link(g.memset(ones_b[:, :], 1.0))
            ch.link(g.affine_select(out=before[:, :], in_=ones_b[:, :], compare_op=ALU.is_ge, fill=0.0,
                                    base=-1, pattern=[[1, P]], channel_multiplier=-1))
            for tile, pat in ((iota_x, [[1, NX]]),):
                ch.link(g.iota(tile[:, :], pattern=pat, base=0, channel_multiplier=0,
                               allow_small_or_imprecise_dtypes=True))
            ch.link(g.iota(pair_id[:, :], pattern=[[2 * P, NT], [1, 2]], base=1, channel_multiplier=2,
                           allow_small_or_imprecise_dtypes=True))
            ch.link(g.affine_select(out=valid[:, :], in_=ones_f[:, 0:1], compare_op=ALU.is_ge, fill=0.0,
                                    base=LAST - 1, pattern=[[0, 1]], channel_multiplier=-1))
            ch.link(g.memset(ft4[:, :, :, D:D1].rearrange("p t h e -> p (t h) e"), 1.0))
            pool.sem_inc(const2_ready, 1)

            pool.wait_ge(far_ready, 1)
            g.partition_all_reduce(far_all[:, :], far[:, :], P, RMAX).then_inc(far_all_ready, 1)
            pool.wait_ge(red_ready, 3)
            g.partition_all_reduce(allr[:, :], red[:, :], P, RMAX).then_inc(allr_ready, 1)

            pool.wait_ge(e_ready, 1)
            pool.wait_ge(ft_ready, 2 * NT)
            pool.wait_ge(flag2_ready, 1)
            with pool.If(pool.value_load(flags[0:1, 1:2]) < 1):
                with pool.Fori(0, H // 2) as hh:
                    for s in range(2):
                        h = hh * 2 + s
                        pool.wait_ge(xp_ready, h + 1)
                        for b in range(2):
                            g.tensor_tensor(x12[:, :, b, :], ft4[:, :, bass.ds(h, 1), :].squeeze(2),
                                            e12[:, b, :, bass.ds(h, 1)].broadcast_to([P, NT, D1]), ALU.mult)\
                                .then_inc(x_made, 1)
                        pool.wait_ge(hi_ready, h + 1)
                        g.tensor_tensor(x12, x12, xp[s][:, :, 0], ALU.subtract).then_inc(rest_made, 1)
                        pool.wait_ge(mid_ready, h + 1)
                        g.tensor_tensor(xp[s][:, :, 2], x12, xp[s][:, :, 1], ALU.subtract).then_inc(xp_ready, 1)

            pool.wait_ge(slots_ready, 1)
            for i in range(2):
                pool.wait_ge(h2_out[i], 16 * (NT // 2))
            pool.wait_ge(h2_turned, 2 + NT)
            for i in range(2):
                g.memset(xg[i], 0.0).then_inc(xg_zeroed, 1)
            pool.wait_ge(xg_zeroed, 2)

            token_bound = pool.to_reg(NP - 1)
            row_bound = pool.to_reg(2 * NP - 1)

            def gather(e, b):
                ch.link(g.tensor_copy(gi[b][:, :], at_col(slot_g, e)))
                pool.sem_inc(gathers_begun, 1)
                g.indirect_dma_start(xg[b], None, h2_dram, bass.IndirectOffsetOnAxis(gi[b][:, 0:1], 0),
                                     bounds_check=token_bound, oob_is_err=False).then_inc(xg_in[b], 16)

            def scatter(e, b):
                ch.link(g.tensor_copy(so[b][:, :], at_col(slot_s, e)))
                pool.wait_ge(ya_ready, e + 1)
                pool.wait_ge(yd_ready, e + 1)
                pool.sem_inc(scatters_begun, 1)
                g.indirect_dma_start(y_dram, bass.IndirectOffsetOnAxis(so[b][:, 0:1], 0), ys[b], None,
                                     bounds_check=row_bound, oob_is_err=False).then_inc(y_out[b], 16)

            gather(0, 0)
            gather(1, 1)

            def pair(q, last):
                for b in range(2):
                    e = q * 2 + b
                    if not last:
                        pool.wait_ge(xg_turned, e + 1)
                        gather(e + 2, b)
                    pool.wait_ge(y_out[b], q * 16)
                    scatter(e, b)

            pool.wait_ge(rank_max_ready, 1)
            g.partition_all_reduce(rank_all[:, :], rank_max[:, :], P, RMAX).then_inc(rank_all_ready, 1)
            run(pool, NX // 2, pair, ch, 4, first=True)
            pool.wait_ge(flag3_ready, 1)
            with pool.If(pool.value_load(flags[0:1, 2:3]) > 0):
                g.iota(iota_o, pattern=[[1, OT]], base=0, channel_multiplier=0,
                       allow_small_or_imprecise_dtypes=True).then_inc(extra_step, 1)
                pool.wait_ge(y_out[0], NX // 2 * 16)
                with pool.Fori(0, OT) as j:
                    pool.wait_ge(extra_step, j * XK + (X0 + 1))
                    g.tensor_copy(gi[0][:, :], at_col(ov_g, j)).then_inc(extra_step, 1)
                    pool.wait_ge(extra_step, j * XK + (X0 + 2))
                    g.tensor_copy(so[0][:, :], at_col(ov_s, j)).then_inc(extra_step, 1)
                    pool.wait_ge(extra_step, j * XK + (X0 + 3))
                    pool.sem_inc(gathers_begun, 1)
                    g.indirect_dma_start(xg[0], None, h2_dram, bass.IndirectOffsetOnAxis(gi[0][:, 0:1], 0),
                                         bounds_check=token_bound, oob_is_err=False).then_inc(ex_in_x, 16)
                    pool.wait_ge(extra_step, j * XK + (X0 + XK - 1))
                    pool.sem_inc(scatters_begun, 1)
                    g.indirect_dma_start(y_dram, bass.IndirectOffsetOnAxis(so[0][:, 0:1], 0), ys[0], None,
                                         bounds_check=row_bound, oob_is_err=False).then_inc(ex_out, 16)
                    pool.wait_ge(ex_out, j * 16 + 16)
                    pool.sem_inc(extra_step, 2)

        @block.vector
        def _(dve):
            v = nc.vector
            ch = Chain(dve, dve_chain)
            link = ch.link
            dve.sem_inc(window_added, WRING)
            dve.sem_inc(compared, 2 * NT)
            dve.sem_inc(sums_added, SRING)
            dve.wait_ge(edges_in, 16 * 6)
            v.tensor_copy(edges_f[:, 0:2, :], edges[:, 0:2, :]).then_inc(edges_float, 1)
            v.tensor_copy(edges_f[0:ET1, 2:4, :], edges[0:ET1, 2:4, :]).then_inc(edges_float, 1)
            dve.wait_ge(edges_float, 2)
            v.tensor_reduce(tmin[:, 0:1], edges_f[:, 1, :], AX.X, ALU.min).then_inc(edges_float, 1)
            v.tensor_reduce(tmin[0:ET1, 1:2], edges_f[0:ET1, 3, :], AX.X, ALU.min).then_inc(edges_float, 1)
            dve.wait_ge(edges_turned, 1)
            link(v.tensor_copy(lo_row[0:1, :], banks[1][0:1, 0:ETP]))
            link(v.tensor_reduce(lo_min[0:1, :], lo_row[0:1, :].rearrange("p (g k) -> p g k", k=GSIZE),
                                 AX.X, ALU.min))
            v.tensor_copy(lo_int[0:1, :], lo_min[0:1, :]).then_inc(lo_ready, 1)
            link(v.tensor_copy(sd_t[:, :, :], banks[0][:, 0:2 * ETP].rearrange("p (k t) -> p k t", k=2)))
            link(v.tensor_copy(si[:, :], sd_t[:, 0, :]))
            link(v.tensor_single_scalar(jt_i[:, :], si[:, :], 7, ALU.logical_shift_right))
            link(v.tensor_single_scalar(jp_i[:, :], si[:, :], P - 1, ALU.bitwise_and))
            link(v.tensor_copy(jt_f[:, :], jt_i[:, :]))
            link(v.tensor_copy(jp_h[:, :], jp_i[:, :]))
            dve.wait_ge(lo_spread, 1)
            link(v.tensor_tensor(dd[:, :].rearrange("p (g k) -> p g k", k=GSIZE),
                                 sd_t[:, 1, :].rearrange("p (g k) -> p g k", k=GSIZE),
                                 banks[2][:, 0:NG].unsqueeze(2).broadcast_to([P, NG, GSIZE]), ALU.subtract))
            link(v.tensor_scalar(pen[:, :], dd[:, :], float(WIN), FAR, ALU.is_ge, ALU.mult))
            link(v.scalar_tensor_tensor(key[:, :], jt_f[:, :], float(WIN), dd[:, :], ALU.mult, ALU.add))
            v.tensor_reduce(far[:, :], pen[:, :], AX.X, ALU.max).then_inc(far_ready, 1)
            v.tensor_tensor(key[:, :], key[:, :], pen[:, :], ALU.add).then_inc(key_ready, 1)
            dve.wait_ge(bd_turned, 1)
            v.tensor_copy(bd[:, :, :], banks[3][:, 0:2 * P].rearrange("p (k n) -> p k n", k=2)).then_inc(bd_ready, 1)
            dve.wait_ge(bda_done, 1)
            v.tensor_copy(bda[:, :, :], banks[4][:, 0:C6 * 2 * H].rearrange("p (c n) -> p c n", c=C6))\
                .then_inc(bda_ready, 1)
            dve.wait_ge(key_ready, 1)
            dve.wait_ge(lo_ready, 1)
            dve.wait_ge(const_ready, 1)

            def one_hot_rows(q, part):
                n = CRING // 2
                r0 = part * n
                dve.wait_ge(window_done, q * WSTEP + (part + 1) * (WSTEP // 2))
                v.tensor_tensor(oha[:, r0:r0 + n, :], iota_p[:, :].unsqueeze(1).broadcast_to([P, n, P]),
                                (jp_h[:, q * CRING + r0:q * CRING + r0 + n] if isinstance(q, int) else
                                 jp_h[:, bass.ds(q * CRING + r0, n)]).unsqueeze(2).broadcast_to([P, n, P]),
                                ALU.is_equal).then_inc(oha_ready, n)

            def one_hot_columns(q, part, i):
                r = part * CRING // 2 + i
                v.tensor_scalar(ohb[:, r, :], iota_k[:, :], at_col(key, q * CRING + r), None,
                                ALU.is_equal).then_inc(ohb_ready, 1)

            def add_window(q, part, i):
                w = part * WSTEP // 2 + i
                gq = q * WSTEP + w
                lo = dve.value_load(at_col(lo_int[0:1, :], gq), min_val=0, max_val=N - 1)
                dve.wait_ge(window_done, gq + (WSTEP + 1))
                dve.wait_ge(window_added, gq + WRING)
                v.tensor_tensor(c32[:, :, bass.ds(lo, WIN)], c32[:, :, bass.ds(lo, WIN)],
                                banks[w % WRING][:, 0:KW].rearrange("p (t n) -> p t n", t=NT), ALU.add)\
                    .then_inc(window_added, 1)

            def windows(q, last):
                for part in range(2):
                    q1, p1 = (q, 1) if part == 0 else (q + 1, 0)
                    more = not (last and part == 1)
                    if more:
                        one_hot_rows(q1, p1)
                        one_hot_columns(q1, p1, 0)
                    add_window(q, part, 0)
                    if more:
                        one_hot_columns(q1, p1, 1)
                        one_hot_columns(q1, p1, 2)
                    add_window(q, part, 1)
                    if more:
                        one_hot_columns(q1, p1, 3)

            def norm(t, xin, hout, var_ready, sd_ready, done):
                for i in range(2):
                    link(v.bn_stats(bns[:, i, :], xin[:, i * F // 2:(i + 1) * F // 2]))
                dve.wait_ge(done, t)
                link(v.bn_aggr(mv[:, :], bns[:, :, :]))
                v.tensor_scalar(ve[:, :], mv[:, 1:2], LN_EPS, None, ALU.add).then_inc(var_ready, 1)
                dve.wait_ge(sd_ready, t + 1)
                link(v.reciprocal(rstd[:, :], sd[:, :]))
                v.tensor_scalar(hout, xin, mv[:, 0:1], rstd[:, 0:1], ALU.subtract, ALU.mult).then_inc(done, 1)

            def norm1(t, s, q):
                dve.wait_ge(x_in[s], q * 16 + 16)
                dve.wait_ge(h_turned, t + 1)
                norm(t, xt[s], ht[s], var1_ready, sd1_ready, h_ready)

            def copy_sums(t):
                s = t % 2
                if t >= 2:
                    dve.wait_ge(res_out[s], t // 2 * 16)
                dve.wait_ge(ft_done, t * 2 + 2)
                v.tensor_copy(rt[s][:, 0:512], banks[4][:, :]).then_inc(res_copied, 1)
                v.tensor_copy(rt[s][:, 512:F], banks[5][:, 0:F - 512]).then_inc(res_copied, 1)
                v.tensor_copy(a12[:, t], banks[5][:, 256:256 + 2 * H]).then_inc(res_copied, 1)

            one_hot_rows(0, 0)
            for i in range(CRING // 2):
                one_hot_columns(0, 0, i)
            norm1(0, 0, 0)
            dve.wait_ge(counts_zeroed, 1)
            QT = ETP // CRING // NT
            assert QT == 2 and QT * NT * CRING == ETP
            for t in range(NT):
                with dve.Fori(QT * t, QT * t + 1) as q:
                    windows(q, False)
                if t < NT - 1:
                    norm1(t + 1, (t + 1) % 2, (t + 1) // 2)
                if t < NT - 1:
                    with dve.Fori(QT * t + 1, QT * t + 2) as q:
                        windows(q, False)
                else:
                    windows(QT * t + 1, True)
                if t >= 1:
                    copy_sums(t - 1)
            copy_sums(NT - 1)
            dve.wait_ge(window_added, NG + WRING)
            dve.wait_ge(far_all_ready, 1)
            v.tensor_copy(flags[0:1, 0:1], far_all[0:1, :]).then_inc(flag1_ready, 1)
            dve.wait_ge(flag1_ready, 1)

            with dve.If(dve.value_load(flags[0:1, 0:1]) > 0):
                with dve.Fori(0, MORE) as p_:
                    n = p_ * MK
                    for i, make in enumerate((
                            lambda: v.tensor_scalar(dd, dd, float(WIN), None, ALU.subtract),
                            lambda: v.tensor_scalar(lo_min[0:1, :], lo_min[0:1, :], float(WIN), float(N),
                                                    ALU.add, ALU.min),
                            lambda: v.tensor_copy(lo_int[0:1, :], lo_min[0:1, :]),
                            lambda: v.tensor_scalar(pen, dd, float(WIN), FAR, ALU.is_ge, ALU.mult),
                            lambda: v.tensor_scalar(pen2, dd, 0.0, FAR, ALU.is_lt, ALU.mult),
                            lambda: v.scalar_tensor_tensor(key[:, :], jt_f, float(WIN), dd, ALU.mult, ALU.add),
                            lambda: v.tensor_tensor(pen, pen, pen2, ALU.add),
                            lambda: v.tensor_tensor(key[:, :], key[:, :], pen, ALU.add))):
                        dve.wait_ge(more_step, n + (i + 1))
                        make().then_inc(more_step, 1)
                    with dve.Fori(0, NG) as gq:
                        m = n + gq * 5
                        dve.wait_ge(more_step, m + 9)
                        v.tensor_tensor(oha[:, 0:GSIZE, :], iota_p[:, :].unsqueeze(1).broadcast_to([P, GSIZE, P]),
                                        jp_h[:, bass.ds(gq * GSIZE, GSIZE)].unsqueeze(2)
                                        .broadcast_to([P, GSIZE, P]), ALU.is_equal).then_inc(more_step, 1)
                        for r in range(GSIZE):
                            v.tensor_scalar(ohb[:, r, :], iota_k[:, :], at_col(key, gq * GSIZE + r), None,
                                            ALU.is_equal).then_inc(more_step, 1)
                        lo = dve.value_load(at_col(lo_int[0:1, :], gq), min_val=0, max_val=N)
                        dve.wait_ge(more_step, m + 13)
                        v.tensor_tensor(c32[:, :, bass.ds(lo, WIN)], c32[:, :, bass.ds(lo, WIN)],
                                        banks[0][:, 0:KW].rearrange("p (t n) -> p t n", t=NT), ALU.add)\
                            .then_inc(more_step, 1)
                dve.wait_ge(more_step, 1 + MORE * MK)
            v.tensor_reduce(red[:, 2:3], c32[:, :, 0:NP], AX.XY, ALU.max).then_inc(red_ready, 1)
            v.tensor_copy(cbf, c32[:, :, 0:NP]).then_inc(counts_ready, 1)

            dve.wait_ge(res_copied, 3 * NT)
            v.tensor_reduce(red[:, 0:1], a12[:, :, 0:H], AX.XY, ALU.max).then_inc(red_ready, 1)
            link(v.tensor_scalar(na1[:, :, :], a12[:, :, 0:H], -1.0, None, ALU.mult))
            v.tensor_reduce(red[:, 1:2], na1[:, :, :], AX.XY, ALU.max).then_inc(red_ready, 1)
            dve.wait_ge(allr_ready, 1)
            link(v.tensor_scalar(nA[:, 0:1], allr[:, 0:1], -1.0, None, ALU.mult))
            link(v.tensor_scalar(nA[:, 1:2], allr[:, 0:1], -SLOPE, None, ALU.mult))
            link(v.tensor_scalar(sA[:, :, :], a12[:, :, H:2 * H], allr[:, 0:1], None, ALU.add))
            link(v.tensor_scalar(fa[:, 0], sA[:, :, :], 1.0 - SLOPE, 0.0, ALU.mult, ALU.min))
            v.tensor_scalar(fa[:, 1], sA[:, :, :], SLOPE - 1.0, 0.0, ALU.mult, ALU.min).then_inc(fa_ready, 1)
            dve.wait_ge(small_turned, 1)
            v.tensor_copy(gateT[:, :, :], banks[3][:, 0:C6 * NX].rearrange("p (c n) -> p c n", c=C6))\
                .then_inc(smallT_ready, 1)
            v.tensor_copy(bT[:, :, :, :].rearrange("p k c n -> p (k c n)"),
                          banks[3][:, C6 * NX:C6 * NX + 3 * HC * NX]).then_inc(smallT_ready, 1)
            link(v.tensor_tensor(flag_f[:, 0:1], allr[0:1, 0:1], allr[0:1, 1:2], ALU.add))
            link(v.tensor_scalar(flag_f[:, 1:2], flag_f[:, 0:1], MAX_RANGE, None, ALU.is_gt))
            link(v.tensor_scalar(flag_f[:, 2:3], allr[0:1, 2:3], MAX_COUNT, None, ALU.is_gt))
            link(v.tensor_tensor(flag_f[:, 3:4], flag_f[:, 1:2], flag_f[:, 2:3], ALU.max))
            v.tensor_copy(flags[0:1, 1:2], flag_f[:, 3:4]).then_inc(flag2_ready, 1)
            dve.wait_ge(flag2_ready, 1)
            dve.wait_ge(e_ready, 1)
            dve.wait_ge(counts_ready, 1)
            for i in range(2):
                dve.wait_ge(res_out[i], 16 * (NT // 2))

            def masks(h, i, add):
                lo, hi = ITS[i]
                dve.wait_ge(a2b_ready, h * 4 + (2 if i == 0 else 4))
                dve.wait_ge(sums_done, h * NT + (ITS[0][1] if i == 0 else NT))
                for jt in range(NT):
                    v.scalar_tensor_tensor(mask[i][:, jt, :], a2b[:, lo * P:hi * P], at_col(na1[:, jt, :], h),
                                           cbf[:, jt, lo * P:hi * P], ALU.is_ge, ALU.mult).then_inc(compared, 1)
                    if jt in (4, 7, 9):
                        add((4, 7, 9).index(jt))
                dve.wait_ge(compared, h * (2 * NT) + (2 * NT + (i + 1) * NT))
                v.tensor_tensor(nmask[i][:, NEG:NT], mask[i][:, NEG:NT], cbf[:, NEG:NT, lo * P:hi * P],
                                ALU.subtract).then_inc(mask_ready, 1)
                add(3)
                add(4)

            def add_sum(h, s, t):
                r = (s * NT + t) % SRING
                dve.wait_ge(t2_ready, h * NT + (t + 1))
                v.scalar_tensor_tensor(at_mid(agg4[:, t], h), banks[r][:, 0:D1], at_col(f12[:, 0, t, :], h),
                                       t2[:, r, :], ALU.mult, ALU.subtract).then_inc(sums_added, 1)

            def heads(hh, last):
                for s in range(2):
                    h = hh * 2 + s
                    masks(h, 1, lambda t: add_sum(h, s, t))
                    if last and s == 1:
                        for t in range(NT // 2, NT):
                            add_sum(h, s, t)
                    else:
                        masks(h + 1, 0, lambda t: add_sum(h, s, NT // 2 + t))

            wide = dve.value_load(flags[0:1, 1:2])
            with dve.If(wide < 1):
                for i, (lo, hi) in enumerate(ITS):
                    v.tensor_scalar(nmask[i][:, 0:NEG], cbf[:, 0:NEG, lo * P:hi * P], -1.0, None, ALU.mult)\
                        .then_inc(neg_ready, 1)
                masks(0, 0, lambda jt: None)
                run(dve, H // 2, heads)
                dve.wait_ge(sums_added, SRING + H * NT)
            with dve.Else():
                with dve.Fori(0, NT) as t:
                    n = t * WT + W0
                    dve.wait_ge(wide_step, n + 1)
                    v.tensor_copy(c_in, c32[:, :, bass.ds(t * P, P)]).then_inc(wide_step, 1)
                    dve.wait_ge(wide_step, n + 3)
                    for i in range(3):
                        m = min(512, NP - 512 * i)
                        v.tensor_copy(c_row[:, 512 * i:512 * i + m], banks[i][:, 0:m]).then_inc(wide_step, 1)
                    dve.wait_ge(wide_step, n + 6)
                    v.tensor_scalar(none_row, c_row, 0.0, -3e38, ALU.is_equal, ALU.mult).then_inc(wide_step, 1)
                    with dve.Fori(0, H) as h:
                        c = n + h * WH + 7
                        dve.wait_ge(wide_step, c + 2)
                        for i in range(3):
                            m = min(512, NP - 512 * i)
                            v.tensor_scalar(e_row[:, 512 * i:512 * i + m], banks[3 + i][:, 0:m],
                                            a12[:, bass.ds(t, 1), bass.ds(h + H, 1)].squeeze(1), None, ALU.add)\
                                .then_inc(wide_step, 1)
                        dve.wait_ge(wide_step, c + 5)
                        v.scalar_tensor_tensor(e_row, e_row, SLOPE, e_row, ALU.mult, ALU.max)\
                            .then_inc(wide_step, 1)
                        dve.wait_ge(wide_step, c + 6)
                        v.tensor_tensor(p_row, e_row, none_row, ALU.add).then_inc(wide_step, 1)
                        dve.wait_ge(wide_step, c + 7)
                        v.tensor_reduce(m_row[:, :], p_row, AX.X, ALU.max).then_inc(wide_step, 1)
                        dve.wait_ge(wide_step, c + 8)
                        v.tensor_scalar(e_row, e_row, m_row[:, 0:1], 0.0, ALU.subtract, ALU.min)\
                            .then_inc(wide_step, 1)
                        dve.wait_ge(wide_step, c + 10)
                        v.tensor_tensor(p_row, e_row, c_row, ALU.mult).then_inc(wide_step, 1)
                        dve.wait_ge(wide_step, c + 12)
                        for i in range(3):
                            m = min(4, NT - 4 * i)
                            v.tensor_copy(p_t[:, 4 * i:4 * i + m, :],
                                          banks[i][:, 0:m * P].rearrange("p (t n) -> p t n", t=m))\
                                .then_inc(wide_step, 1)
                        dve.wait_ge(wide_step, c + 16)
                        v.tensor_copy(agg4[:, bass.ds(t, 1), bass.ds(h, 1), :].squeeze(1).squeeze(1),
                                      duo[:, 0, 0:D1]).then_inc(wide_step, 1)
                dve.wait_ge(wide_step, 1 + W0 + NT * WT)
            dve.sem_inc(attention_done, 1)
            link(v.tensor_scalar(rden[:, :, :], agg4[:, :, :, D], 1e-37, None, ALU.max))
            link(v.reciprocal(rden[:, :, :], rden[:, :, :]))

            def x1_norm(t, s, q):
                bt = at_mid(base, t)
                dve.wait_ge(xr_in[s], q * 32 + 32)
                link(v.tensor_tensor(bt.rearrange("p (h e) -> p h e", h=H), at_mid(agg4, t)[:, :, 0:D],
                                     at_mid(rden, t).unsqueeze(2).broadcast_to([P, H, D]), ALU.mult))
                link(v.tensor_tensor(bt, bt, xres[1][s], ALU.add))
                v.scalar_tensor_tensor(bt, bt, 0.0, xres[0][s], ALU.max, ALU.add).then_inc(x1_ready, 1)
                dve.wait_ge(x1_ready, t + 1)
                dve.wait_ge(h2_turned, t + 1)
                dve.wait_ge(h2_out[s], q * 16)
                norm(t, bt, xg[s], var2_ready, sd2_ready, h2_ready)

            def tiles2(q, last):
                for s in range(2):
                    t = q * 2 + s
                    if s == 0:
                        x1_norm(t + 1, 1, q)
                    elif not last:
                        x1_norm(t + 1, 0, q + 1)
                    dve.wait_ge(logits_done, t + 1)
                    v.tensor_copy(at_mid(lg, t), banks[4 + s][:, 0:NX]).then_inc(logits_read, 1)

            x1_norm(0, 0, 0)
            for q in range(NT // 2):
                tiles2(q, q == NT // 2 - 1)

            dve.wait_ge(logits_read, NT)
            for t in range(NT):
                link(v.max(mx8[:, t, :], lg[:, t, :]))
                link(v.max_index(ix8[:, t, :], mx8[:, t, :], lg[:, t, :]))
            v.tensor_tensor(ex[:, :, :], lg[:, :, :], mx8[:, :, 0:1].broadcast_to([P, NT, NX]), ALU.subtract)\
                .then_inc(ex_lg, 1)
            v.tensor_tensor(ex1[:, :], mx8[:, :, 1], mx8[:, :, 0], ALU.subtract).then_inc(ex_in, 1)
            link(v.tensor_copy(ixf[:, :, :], ix8[:, :, 0:2]))
            for k in range(2):
                link(v.tensor_tensor(mk[:, :, k, :], iota_x[:, :].unsqueeze(1).broadcast_to([P, NT, NX]),
                                     ixf[:, :, k:k + 1].broadcast_to([P, NT, NX]), ALU.is_equal))
            link(v.tensor_scalar(mk[:, NT - 1], mk[:, NT - 1], valid[:, 0:1], None, ALU.mult))
            link(v.tensor_tensor(msum[:, :, :], mk[:, :, 0, :], mk[:, :, 1, :], ALU.add))
            link(v.memset(macc[:, 0, :], 0.0))
            for t in range(1, NT):
                link(v.tensor_tensor(macc[:, t, :], macc[:, t - 1, :], msum[:, t - 1, :], ALU.add))
            dve.sem_inc(m_ready, 1)
            dve.wait_ge(ex_ready, 1)
            link(v.tensor_reduce(pr[:, 0, :], ex[:, :, :], AX.X, ALU.add))
            link(v.reciprocal(pr[:, 0, :], pr[:, 0, :]))
            link(v.tensor_tensor(pr[:, 1, :], ex1[:, :], pr[:, 0, :], ALU.mult))
            link(v.tensor_tensor(psum_pr[:, :], pr[:, 0, :], pr[:, 1, :], ALU.add))
            link(v.tensor_scalar(psum_pr[:, :], psum_pr[:, :], 1e-20, None, ALU.add))
            link(v.reciprocal(psum_pr[:, :], psum_pr[:, :]))
            for k in range(2):
                link(v.tensor_tensor(wk[:, :, k], pr[:, k, :], psum_pr[:, :], ALU.mult))
                link(v.tensor_tensor(slb[:, :, k, 0, :], mk[:, :, k, :],
                                     pair_id[:, :].rearrange("p (t k) -> p t k", k=2)[:, :, k:k + 1]
                                     .broadcast_to([P, NT, NX]), ALU.mult))
                link(v.tensor_tensor(slb[:, :, k, 1, :], mk[:, :, k, :],
                                     wk[:, :, k:k + 1].broadcast_to([P, NT, NX]), ALU.mult))
            v.tensor_tensor(gm[:, :, :], slb[:, :, 0, 1, :], slb[:, :, 1, 1, :], ALU.add).then_inc(gm_ready, 1)
            dve.wait_ge(rank_done, 2)
            link(v.tensor_copy(n_all[:, :], banks[4][:, 0:NX]))
            link(v.tensor_copy(rk[:, :, :], banks[0][:, 0:NT * NX].rearrange("p (t n) -> p t n", t=NT)))
            for k in range(2):
                link(v.tensor_tensor(rkm[:, :, :], mk[:, :, k, :], rk[:, :, :], ALU.mult))
                link(v.tensor_reduce(rank[:, :, k], rkm[:, :, :], AX.X, ALU.add))
            v.tensor_reduce(rank_max[:, :], rank[:, :, :], AX.XY, ALU.max).then_inc(rank_max_ready, 1)
            for n in range(2 * NT):
                if n >= 4:
                    dve.wait_ge(slots_done, n - 3)
                v.tensor_scalar(sla[:, n % 4, :], iota_p[:, :], rank[:, n // 2, n % 2:n % 2 + 1], None,
                                ALU.is_equal).then_inc(sl_ready, 1)
            dve.wait_ge(slots_done, 2 * NT)
            link(v.tensor_copy(slot_v[:, :, :], banks[0][:, 0:2 * NX].rearrange("p (k n) -> p k n", k=2)))
            link(v.tensor_scalar(slot_f[:, :], slot_v[:, 0, :], 0.0, 8193.0, ALU.is_equal, ALU.mult))
            link(v.tensor_tensor(slot_f[:, :], slot_f[:, :], slot_v[:, 0, :], ALU.add))
            link(v.tensor_scalar(slot_f[:, :], slot_f[:, :], 1.0, None, ALU.subtract))
            link(v.tensor_copy(slot_s[:, :], slot_f[:, :]))
            v.tensor_single_scalar(slot_g[:, :], slot_s[:, :], 1, ALU.logical_shift_right).then_inc(slots_ready, 1)
            dve.wait_ge(rank_all_ready, 1)
            link(v.tensor_scalar(flag_f[:, 0:1], rank_all[0:1, :], float(P), None, ALU.is_ge))
            v.tensor_copy(flags[0:1, 2:3], flag_f[:, 0:1]).then_inc(flag3_ready, 1)
            for t in range(NT):
                dve.wait_ge(bias_done, 2 * t + 2)
                for i in range(2):
                    src_bank = duo[:, i, 0:F // 2] if t % 2 == 0 else banks[4 + i][:, 0:F // 2]
                    v.tensor_tensor(base[:, t, i * F // 2:(i + 1) * F // 2],
                                    base[:, t, i * F // 2:(i + 1) * F // 2], src_bank, ALU.add)\
                        .then_inc(base_ready, 1)

            def turn(e, b):
                dve.wait_ge(xg_turned, e + 1)
                v.tensor_copy(xgT[b][:, 3:6, :], duo[:, 1, 0:3 * P].rearrange("p (c n) -> p c n", c=3))\
                    .then_inc(xgT_d, 1)

            def group(q, last):
                for s in range(WSLOTS):
                    e, b = q * WSLOTS + s, s % 2
                    if not (last and s == WSLOTS - 1):
                        turn(e + 1, 1 - b)
                    for m in range(HC):
                        dve.wait_ge(l3_done, e * 2 + (m + 1))
                        v.tensor_scalar(hid[2][b][:, m, :], banks[2 + m][:, 0:P], at_col(bT[:, 2, m, :], e),
                                        None, ALU.add).then_inc(z_ready, 1)
                    dve.wait_ge(l4_done, e + 1)
                    dve.wait_ge(y_out[b], q * 32 + 16 * (s // 2))
                    v.tensor_scalar(ys[b][:, F // 2:F], banks[5][:, 0:F // 2], at_col(slot_v[:, 1, :], e),
                                    None, ALU.mult).then_inc(yd_ready, 1)

            turn(0, 0)
            run(dve, NX // WSLOTS, group, first=True)
            with dve.If(dve.value_load(flags[0:1, 2:3]) > 0):
                step = [1]

                def then(ins):
                    ins.then_inc(extra_step, 1)
                    step[0] += 1
                    dve.wait_ge(extra_step, step[0])

                dve.wait_ge(extra_step, 1)
                then(v.tensor_single_scalar(ov_n, n_all[:, :], float(P - 1), ALU.add))
                then(v.tensor_copy(ov_ni, ov_n))
                then(v.tensor_single_scalar(ov_ni, ov_ni, 7, ALU.logical_shift_right))
                then(v.tensor_copy(ov_n, ov_ni))
                then(v.tensor_scalar(ov_n, ov_n, 1.0, 0.0, ALU.subtract, ALU.max))
                then(v.tensor_copy(ov_end[:, 0:1], ov_n[:, 0:1]))
                for i in range(1, NX):
                    then(v.tensor_tensor(ov_end[:, i:i + 1], ov_end[:, i - 1:i], ov_n[:, i:i + 1], ALU.add))
                then(v.tensor_tensor(ov_first, ov_end, ov_n, ALU.subtract))
                both = [P, OT, NX]
                then(v.tensor_tensor(ov_tab, iota_o.unsqueeze(2).broadcast_to(both),
                                     ov_first.unsqueeze(1).broadcast_to(both), ALU.is_ge))
                then(v.tensor_tensor(ov_tab2, iota_o.unsqueeze(2).broadcast_to(both),
                                     ov_end.unsqueeze(1).broadcast_to(both), ALU.is_lt))
                then(v.tensor_tensor(ov_tab, ov_tab, ov_tab2, ALU.mult))
                then(v.tensor_tensor(ov_tab, ov_tab, iota_x[:, :].unsqueeze(1).broadcast_to(both), ALU.mult))
                then(v.tensor_reduce(ov_ex, ov_tab, AX.X, ALU.add))
                then(v.tensor_copy(ov_exi, ov_ex))
                for k in range(2):
                    then(v.tensor_tensor(ov_m, mk[:, :, k, :],
                                         ov_first.unsqueeze(1).broadcast_to([P, NT, NX]), ALU.mult))
                    then(v.tensor_reduce(ov_base[:, :, k], ov_m, AX.X, ALU.add))
                then(v.tensor_copy(ov_rank_i, rank[:, :, :]))
                then(v.tensor_single_scalar(ov_hi_i, ov_rank_i, 7, ALU.logical_shift_right))
                then(v.tensor_single_scalar(ov_lo_i, ov_rank_i, P - 1, ALU.bitwise_and))
                then(v.tensor_copy(ov_hi, ov_hi_i))
                then(v.tensor_copy(ov_lo, ov_lo_i))
                then(v.tensor_scalar(ov_ge, ov_hi, 1.0, None, ALU.is_ge))
                then(v.tensor_tensor(ov_hi, ov_hi, ov_base, ALU.add))
                then(v.tensor_tensor(ov_hi, ov_hi, ov_ge, ALU.mult))
                then(v.tensor_scalar(ov_hi, ov_hi, 1.0, None, ALU.subtract))
                for i in range(2 * NT):
                    t, k = i // 2, i % 2
                    then(v.tensor_scalar(ov_a, iota_p[:, :], ov_lo[:, t, k:k + 1], None, ALU.is_equal))
                    then(v.tensor_scalar(ov_b[:, 0, :], iota_o, ov_hi[:, t, k:k + 1], pair_id[:, i:i + 1],
                                         ALU.is_equal, ALU.mult))
                    v.tensor_scalar(ov_b[:, 1, :], iota_o, ov_hi[:, t, k:k + 1], wk[:, t, k:k + 1],
                                    ALU.is_equal, ALU.mult).then_inc(extra_step, 1)
                    step[0] += 2
                    dve.wait_ge(extra_step, step[0])
                then(v.tensor_copy(ov_v, banks[0][:, 0:2 * OT].rearrange("p (k n) -> p k n", k=2)))
                then(v.tensor_scalar(ov_f, ov_v[:, 0, :], 0.0, FAR + 1.0, ALU.is_equal, ALU.mult))
                then(v.tensor_tensor(ov_f, ov_f, ov_v[:, 0, :], ALU.add))
                then(v.tensor_scalar(ov_f, ov_f, 1.0, None, ALU.subtract))
                then(v.tensor_copy(ov_s, ov_f))
                then(v.tensor_single_scalar(ov_g, ov_s, 1, ALU.logical_shift_right))
                assert step[0] == X0 + 1, step[0]
                with dve.Fori(0, OT) as j:
                    n = j * XK + (X0 + 1)
                    e = dve.value_load(at_col(ov_exi[0:1, :], j), min_val=0, max_val=NX - 1)
                    dve.wait_ge(extra_step, n + 3)
                    for i in range(2):
                        v.tensor_copy(xgT[0][:, 3 * i:3 * i + 3, :],
                                      duo[:, i, 0:3 * P].rearrange("p (c n) -> p c n", c=3))\
                            .then_inc(extra_step, 1)
                    dve.wait_ge(extra_step, n + 13)
                    for m in range(HC):
                        v.tensor_scalar(hid[2][0][:, m, :], banks[2 + m][:, 0:P], at_col(bT[:, 2, m, :], e),
                                        None, ALU.add).then_inc(extra_step, 1)
                    dve.wait_ge(extra_step, n + 16)
                    for i in range(2):
                        v.tensor_scalar(ys[0][:, i * F // 2:(i + 1) * F // 2], banks[4 + i][:, 0:F // 2],
                                        at_col(ov_v[:, 1, :], j), None, ALU.mult).then_inc(extra_step, 1)
                dve.wait_ge(extra_step, X0 + OT * XK + 1)

            dve.wait_ge(base_ready, 2 * NT)
            for t in range(NT):
                dve.wait_ge(ypair_in[t % YR], 16 * (t // YR + 1))
                for k in range(2):
                    ins = v.tensor_tensor(base[0:rows(t), t, :], base[0:rows(t), t, :],
                                          ypair[t % YR][0:rows(t), F * k:F * (k + 1)], ALU.add)
                    if k == 0:
                        link(ins)
                    else:
                        ins.then_inc(sum_ready, 1)

        @block.scalar
        def _(act):
            a = nc.scalar

            def deviation(t, var_ready, sd_ready):
                act.wait_ge(var_ready, t + 1)
                a.activation(sd[:, :], ve[:, :], ACT.Sqrt).then_inc(sd_ready, 1)

            deviation(0, var1_ready, sd1_ready)

            def tiles1(q, last):
                for s in range(2):
                    t = q * 2 + s
                    if not (last and s == 1):
                        deviation(t + 1, var1_ready, sd1_ready)
                    act.wait_ge(h_turned, t + 3)
                    for i in range(2):
                        a.activation(hTt[s][:, 3 * i:3 * i + 3, :],
                                     duo[:, i, 0:3 * P].rearrange("p (c n) -> p c n", c=3), ACT.Copy)\
                            .then_inc(hT_ready, 1)
                    act.wait_ge(ft_done, t * 2 + 1)
                    a.activation(at_mid(ft4, t)[:, 0:8, 0:D], banks[2][:, :].rearrange("p (h e) -> p h e", e=D),
                                 ACT.Copy).then_inc(ft_ready, 1)
                    a.activation(at_mid(ft4, t)[:, 8:H, 0:D],
                                 banks[3][:, 0:4 * D].rearrange("p (h e) -> p h e", e=D), ACT.Copy)\
                        .then_inc(ft_ready, 1)

            run(act, NT // 2, tiles1)
            act.wait_ge(fa_ready, 1)
            for b in range(2):
                a.activation(e12[:, b], a12[:, :, 0:H], ACT.Exp, bias=nA[:, b:b + 1],
                             scale=1.0 if b == 0 else SLOPE).then_inc(e_made, 1)
            a.activation(f12[:, :, :, :].rearrange("p b t h -> p (b t h)"),
                         fa[:, :, :, :].rearrange("p b t h -> p (b t h)"), ACT.Exp).then_inc(e_made, 1)
            act.wait_ge(a2_turned, 1)
            for i in range(3):
                n = min(512, NP - 512 * i)
                a.activation(a2T[:, 512 * i:512 * i + n], banks[i][0:H, 0:n], ACT.Copy).then_inc(a2T_ready, 1)
            act.wait_ge(e_made, 3)
            act.sem_inc(e_ready, 1)
            act.wait_ge(a2T_ready, 3)

            def pick(h):
                act.wait_ge(a2_spread, h)
                a.activation(a2m[:, :], a2T[:, :], ACT.Copy, scale=at_col(ident[0:H, :], h)).then_inc(a2m_ready, 1)

            def spread0(h):
                act.wait_ge(a2_spread, h + 1)
                act.wait_ge(compared, h * (2 * NT) + NT)
                a.activation(a2b[:, 0:512], banks[4][:, :], ACT.Copy).then_inc(a2b_ready, 1)
                a.activation(a2b[:, 512:PART], duo[:, 0, 0:PART - 512], ACT.Copy).then_inc(a2b_ready, 1)

            def spread1(h):
                act.wait_ge(compared, h * (2 * NT) + 2 * NT)
                a.activation(a2b[:, PART:1024], duo[:, 0, PART - 512:512], ACT.Copy).then_inc(a2b_ready, 1)
                a.activation(a2b[:, 1024:NP], duo[:, 1, 0:NP - 1024], ACT.Copy).then_inc(a2b_ready, 1)

            def high(h, s):
                act.wait_ge(x_made, h * 2 + 2)
                act.wait_ge(sums_done, h * NT)
                a.activation(xp[s][:, :, 0], x12, ACT.Copy).then_inc(hi_ready, 1)

            def middle(h, s):
                act.wait_ge(rest_made, h + 1)
                a.activation(xp[s][:, :, 1], x12, ACT.Copy).then_inc(mid_ready, 1)

            def second_sums(h, s, ts):
                for t in ts:
                    r = (s * NT + t) % SRING
                    act.wait_ge(sums_done, h * NT + (t + 1 + NT))
                    a.activation(t2[:, r, :], banks[r][:, D1:2 * D1], ACT.Copy,
                                 scale=at_col(f12[:, 1, t, :], h)).then_inc(t2_ready, 1)

            def heads(hh, last):
                for s in range(2):
                    h = hh * 2 + s
                    more = not (last and s == 1)
                    if more:
                        spread0(h + 1)
                        high(h + 1, 1 - s)
                    second_sums(h, s, range(0, NT // 2))
                    if more:
                        middle(h + 1, 1 - s)
                        spread1(h + 1)
                        if not (last and s == 0):
                            pick(h + 2)
                    second_sums(h, s, range(NT // 2, NT))

            act.wait_ge(flag2_ready, 1)
            with act.If(act.value_load(flags[0:1, 1:2]) < 1):
                pick(0)
                spread0(0)
                spread1(0)
                pick(1)
                high(0, 0)
                middle(0, 0)
                run(act, H // 2, heads)
            with act.Else():
                act.wait_ge(wide_step, 2)
                for i in range(3):
                    n = min(512, NP - 512 * i)
                    a.activation(a2T[:, 512 * i:512 * i + n], banks[i][0:H, 0:n], ACT.Copy).then_inc(wide_step, 1)
                with act.Fori(0, NT) as t:
                    with act.Fori(0, H) as h:
                        c = t * WT + h * WH + (W0 + 7)
                        act.wait_ge(wide_step, c)
                        a.activation(a2m[:, :], a2T[:, :], ACT.Copy, scale=at_col(ident[0:H, :], h))\
                            .then_inc(wide_step, 1)
                        act.wait_ge(wide_step, c + 9)
                        a.activation(e_row, e_row, ACT.Exp).then_inc(wide_step, 1)

            deviation(0, var2_ready, sd2_ready)

            def tiles2(q, last):
                for s in range(2):
                    t = q * 2 + s
                    if not (last and s == 1):
                        deviation(t + 1, var2_ready, sd2_ready)
                    act.wait_ge(h2_turned, t + 3)
                    for i in range(2):
                        a.activation(xgT[s][:, 3 * i:3 * i + 3, :],
                                     duo[:, i, 0:3 * P].rearrange("p (c n) -> p c n", c=3), ACT.Copy)\
                            .then_inc(h2T_ready, 1)

            run(act, NT // 2, tiles2)
            act.wait_ge(ex_in, 1)
            act.wait_ge(ex_lg, 1)
            a.activation(ex[:, :, :], ex[:, :, :], ACT.Exp).then_inc(ex_made, 1)
            a.activation(ex1[:, :], ex1[:, :], ACT.Exp).then_inc(ex_made, 1)
            act.wait_ge(ex_made, 2)
            act.sem_inc(ex_ready, 1)
            act.wait_ge(gm_turned, 1)
            for i in range(3):
                n = min(512, NP - 512 * i)
                a.activation(gmT[:, 512 * i:512 * i + n], banks[1 + i][0:NX, 0:n], ACT.Copy).then_inc(gmT_ready, 1)

            def turn(e, b):
                act.wait_ge(xg_turned, e + 1)
                a.activation(xgT[b][:, 0:3, :], duo[:, 0, 0:3 * P].rearrange("p (c n) -> p c n", c=3), ACT.Copy)\
                    .then_inc(xgT_a, 1)

            def gelu1(e, b):
                for m in range(HC):
                    act.wait_ge(l1_done, e * 2 + (m + 1))
                    a.activation(hid[0][b][:, m, :], banks[m][:, 0:P], ACT.Gelu,
                                 bias=at_col(bT[:, 0, m, :], e)).then_inc(g1_ready, 1)

            def group(q, last):
                for s in range(WSLOTS):
                    e, b = q * WSLOTS + s, s % 2
                    more = not (last and s == WSLOTS - 1)
                    if more:
                        turn(e + 1, 1 - b)
                    for m in range(HC):
                        act.wait_ge(l2_done, e * 2 + (m + 1))
                        a.activation(hid[1][b][:, m, :], banks[2 + m][:, 0:P], ACT.Gelu,
                                     bias=at_col(bT[:, 1, m, :], e)).then_inc(g2_ready, 1)
                    if more:
                        gelu1(e + 1, 1 - b)
                    act.wait_ge(l4a_done, e + 1)
                    act.wait_ge(y_out[b], q * 32 + 16 * (s // 2))
                    a.activation(ys[b][:, 0:F // 2], banks[4][:, 0:F // 2], ACT.Copy,
                                 scale=at_col(slot_v[:, 1, :], e)).then_inc(ya_ready, 1)

            turn(0, 0)
            gelu1(0, 0)
            run(act, NX // WSLOTS, group, first=True)
            act.wait_ge(flag3_ready, 1)
            with act.If(act.value_load(flags[0:1, 2:3]) > 0):
                with act.Fori(0, OT) as j:
                    n = j * XK + (X0 + 1)
                    act.wait_ge(extra_step, n)
                    e = act.value_load(at_col(ov_exi[0:1, :], j), min_val=0, max_val=NX - 1)
                    for k in range(2):
                        act.wait_ge(extra_step, n + (6 if k == 0 else 9))
                        for m in range(HC):
                            a.activation(hid[k][0][:, m, :], banks[2 * k + m][:, 0:P], ACT.Gelu,
                                         bias=at_col(bT[:, k, m, :], e)).then_inc(extra_step, 1)

        @block.tensor
        def _(pe):
            T = nc.tensor
            pe.sem_inc(window_done, WSTEP)
            pe.sem_inc(h_turned, 2)
            pe.sem_inc(h2_turned, 2)
            pe.sem_inc(sums_done, NT)
            pe.wait_ge(const_ready, 1)

            pe.wait_ge(edges_float, 4)
            for k in range(2):
                T.transpose(banks[0][:, k * ETP:k * ETP + P], edges_f[:, k, :], ident[:, :])
                T.transpose(banks[0][:, k * ETP + P:(k + 1) * ETP], edges_f[0:ET1, 2 + k, :], ident[0:ET1, 0:ET1])
            T.transpose(banks[1][0:1, 0:P], tmin[:, 0:1], ident[:, :])
            T.transpose(banks[1][0:1, P:ETP], tmin[0:ET1, 1:2], ident[0:ET1, 0:ET1]).then_inc(edges_turned, 1)
            pe.wait_ge(gnnw_in, 16 * (4 + 2 * H))
            pe.wait_ge(lo_ready, 1)
            T.matmul(banks[2][:, 0:NG], ones_f[0:1, :], lo_min[0:1, :], start=True, stop=True).then_inc(lo_spread, 1)
            for k in range(2):
                ins = T.transpose(banks[3][:, k * P:(k + 1) * P], bdn[:, k, :], ident[:, :])
            ins.then_inc(bd_turned, 1)
            T.matmul(banks[4][:, 0:C6 * 2 * H], bdn[:, 0, :], at[:, :, :].rearrange("p c n -> p (c n)"),
                     start=True, stop=True).then_inc(bda_done, 1)
            pe.wait_ge(key_ready, 1)
            pe.wait_ge(bd_ready, 1)

            def windows(q):
                for w in range(WSTEP):
                    pe.wait_ge(window_added, q * WSTEP + (w + 1))
                    for k in range(GSIZE):
                        r = w * GSIZE + k
                        pe.wait_ge(oha_ready, q * CRING + (r + 1))
                        pe.wait_ge(ohb_ready, q * CRING + (r + 1))
                        ins = T.matmul(banks[w % WRING][:, 0:KW], oha[:, r, :], ohb[:, r, :],
                                       start=(k == 0), stop=(k == GSIZE - 1))
                    ins.then_inc(window_done, 1)

            pe.wait_ge(bda_ready, 1)

            def transposes(tile, done):
                for c in range(C6):
                    ins = T.transpose(duo[:, c // 3, P * (c % 3):P * (c % 3) + P],
                                      tile(c), ident[:, :])
                ins.then_inc(done, 1)

            def tiles1(q, last):
                for s in range(2):
                    t = q * 2 + s
                    windows(t * 2)
                    pe.wait_ge(h_ready, t + 1)
                    pe.wait_ge(hT_ready, t * 2)
                    transposes(lambda c: ht[s][:, c * P:(c + 1) * P], h_turned)
                    windows(t * 2 + 1)
                    pe.wait_ge(hT_ready, t * 2 + 2)
                    pe.wait_ge(ft_ready, t * 2)
                    for c in range(C6):
                        ins = T.matmul(banks[2 + c // 4][:, P * (c % 4):P * (c % 4) + P], hTt[s][:, c, :],
                                       bd[:, 0, :], start=True, stop=True)
                    ins.then_inc(ft_done, 1)
                    pe.wait_ge(res_copied, t * 3)
                    for c in range(C6):
                        T.matmul(banks[4 + c // 4][:, P * (c % 4):P * (c % 4) + P], hTt[s][:, c, :],
                                 bd[:, 1, :], start=True, stop=True)
                    for c in range(C6):
                        ins = T.matmul(banks[5][:, 256:256 + 2 * H], hTt[s][:, c, :], bda[:, c, :],
                                       start=(c == 0), stop=(c == C6 - 1))
                    ins.then_inc(ft_done, 1)

            run(pe, NT // 2, tiles1, first=True)
            pe.wait_ge(flag1_ready, 1)
            with pe.If(pe.value_load(flags[0:1, 0:1]) > 0):
                pe.sem_inc(more_step, 1)
                with pe.Fori(0, MORE) as p_:
                    with pe.Fori(0, NG) as gq:
                        pe.wait_ge(more_step, p_ * MK + gq * 5 + 12)
                        for k in range(GSIZE):
                            ins = T.matmul(banks[0][:, 0:KW], oha[:, k, :], ohb[:, k, :],
                                           start=(k == 0), stop=(k == GSIZE - 1))
                        ins.then_inc(more_step, 1)
                pe.wait_ge(more_step, 1 + MORE * MK)
            pe.wait_ge(window_added, WRING + NG)
            pe.wait_ge(res_copied, NT * 3)
            pe.wait_ge(ft_ready, NT * 2)
            for t in range(NT):
                ins = T.transpose(banks[t // 4][0:H, P * (t % 4):P * (t % 4) + P], a12[:, t, H:2 * H], ident[:, :])
            ins.then_inc(a2_turned, 1)
            pe.wait_ge(small_in, 16 * 5)
            for c in range(C6):
                T.transpose(banks[3][:, c * NX:(c + 1) * NX], chunks(gate_n[:, :], c), ident[0:NX, 0:NX])
            for k in range(3):
                for c in range(HC):
                    n = (C6 + k * HC + c) * NX
                    ins = T.transpose(banks[3][:, n:n + NX], chunks(bn[:, k, :], c), ident[0:NX, 0:NX])
            ins.then_inc(small_turned, 1)

            def spread(h):
                pe.wait_ge(a2m_ready, h + 1)
                pe.wait_ge(a2b_ready, h * 4)
                T.matmul(banks[4][:, :], ones_f[0:H, :], a2m[:, 0:512], start=True, stop=True)
                T.matmul(duo[:, 0, :], ones_f[0:H, :], a2m[:, 512:1024], start=True, stop=True)
                T.matmul(duo[:, 1, 0:NP - 1024], ones_f[0:H, :], a2m[:, 1024:NP], start=True, stop=True)\
                    .then_inc(a2_spread, 1)

            def heads(hh, last):
                for s in range(2):
                    h = hh * 2 + s
                    if not (last and s == 1):
                        spread(h + 1)
                    pe.wait_ge(xp_ready, h + 2)
                    for i, (lo, hi) in enumerate(ITS):
                        pe.wait_ge(mask_ready, h * 2 + (i + 1))
                        for t in range(lo, hi):
                            r = (s * NT + t) % SRING
                            pe.wait_ge(sums_added, h * NT + (t + 1))
                            cols = slice((t - lo) * P, (t - lo + 1) * P)
                            for jt in range(NT):
                                both = 2 if jt < NEG else 1
                                for k in range(3):
                                    T.matmul(banks[r][:, 0:both * D1], mask[i][:, jt, cols],
                                             xp[s][:, jt, k, 0:both].rearrange("p b e -> p (b e)"),
                                             start=(jt == 0 and k == 0), stop=False)
                            for jt in range(NT):
                                for k in range(3):
                                    ins = T.matmul(banks[r][:, D1:2 * D1], nmask[i][:, jt, cols],
                                                   xp[s][:, jt, k, 1, :], start=False,
                                                   stop=(jt == NT - 1 and k == 2))
                            ins.then_inc(sums_done, 1)

            pe.wait_ge(a2T_ready, 3)
            pe.wait_ge(smallT_ready, 2)
            pe.wait_ge(flag2_ready, 1)
            with pe.If(pe.value_load(flags[0:1, 1:2]) < 1):
                spread(0)
                pe.wait_ge(neg_ready, 2)
                run(pe, H // 2, heads)
            with pe.Else():
                pe.sem_inc(wide_step, 1)
                for t in range(NT):
                    ins = T.transpose(banks[t // 4][0:H, P * (t % 4):P * (t % 4) + P], a12[:, t, 0:H], ident[:, :])
                ins.then_inc(wide_step, 1)
                with pe.Fori(0, NT) as t:
                    n = t * WT + W0
                    pe.wait_ge(wide_step, n + 2)
                    for jt in range(NT):
                        ins = T.transpose(banks[jt // 4][:, P * (jt % 4):P * (jt % 4) + P], c_in[:, jt, :],
                                          ident[:, :])
                    ins.then_inc(wide_step, 1)
                    with pe.Fori(0, H) as h:
                        c = n + h * WH + 7
                        pe.wait_ge(wide_step, c + 1)
                        for i in range(3):
                            m = min(512, NP - 512 * i)
                            ins = T.matmul(banks[3 + i][:, 0:m], ones_f[0:H, :], a2m[:, 512 * i:512 * i + m],
                                           start=True, stop=True)
                        ins.then_inc(wide_step, 1)
                        pe.wait_ge(wide_step, c + 11)
                        for jt in range(NT):
                            ins = T.transpose(banks[jt // 4][:, P * (jt % 4):P * (jt % 4) + P],
                                              p_row[:, jt * P:(jt + 1) * P], ident[:, :])
                        ins.then_inc(wide_step, 1)
                        pe.wait_ge(wide_step, c + 15)
                        for jt in range(NT):
                            ins = T.matmul(duo[:, 0, 0:D1], p_t[:, jt, :], at_mid(ft4[:, jt], h),
                                           start=(jt == 0), stop=(jt == NT - 1))
                        ins.then_inc(wide_step, 1)

            def tiles2(q, last):
                for s in range(2):
                    t = q * 2 + s
                    pe.wait_ge(h2_ready, t + 1)
                    pe.wait_ge(h2T_ready, t * 2)
                    transposes(lambda c: chunks(xg[s], c), h2_turned)
                    pe.wait_ge(h2T_ready, t * 2 + 2)
                    if s == 0:
                        pe.wait_ge(logits_read, q * 2)
                    else:
                        pe.wait_ge(logits_read, q * 2)
                    for c in range(C6):
                        ins = T.matmul(banks[4 + s][:, 0:NX], xgT[s][:, c, :], gateT[:, c, :],
                                       start=(c == 0), stop=(c == C6 - 1))
                    ins.then_inc(logits_done, 1)

            run(pe, NT // 2, tiles2, first=True)
            pe.wait_ge(m_ready, 1)
            T.matmul(banks[0][:, 0:NT * NX], before[:, :], msum[:, :, :].rearrange("p t n -> p (t n)"),
                     start=True, stop=False)
            T.matmul(banks[0][:, 0:NT * NX], ones_b[:, :], macc[:, :, :].rearrange("p t n -> p (t n)"),
                     start=False, stop=True).then_inc(rank_done, 1)
            for k, chosen in enumerate((macc, msum)):
                ins = T.matmul(banks[4][:, 0:NX], ones_b[:, :], chosen[:, NT - 1, :], start=(k == 0), stop=(k == 1))
            ins.then_inc(rank_done, 1)
            pe.wait_ge(gm_ready, 1)
            for t in range(NT):
                ins = T.transpose(banks[1 + t // 4][0:NX, P * (t % 4):P * (t % 4) + P], gm[:, t, :], ident[:, :])
            ins.then_inc(gm_turned, 1)
            for n in range(2 * NT):
                pe.wait_ge(sl_ready, n + 1)
                T.matmul(banks[0][:, 0:2 * NX], sla[:, n % 4, :],
                         slb[:, n // 2, n % 2].rearrange("p k n -> p (k n)"),
                         start=(n == 0), stop=(n == 2 * NT - 1)).then_inc(slots_done, 1)
            pe.wait_ge(gmT_ready, 3)
            pe.wait_ge(logits_read, NT)
            for t in range(NT):
                if t >= 2:
                    pe.wait_ge(base_ready, 2 * (t - 1))
                for i in range(2):
                    dst_bank = duo[:, i, 0:F // 2] if t % 2 == 0 else banks[4 + i][:, 0:F // 2]
                    T.matmul(dst_bank, gmT[:, t * P:(t + 1) * P], bln[:, i * F // 2:(i + 1) * F // 2],
                             start=True, stop=True).then_inc(bias_done, 1)
            pe.wait_ge(base_ready, 2 * NT)

            def turn(e, b, q, half):
                pe.wait_ge(xg_in[b], q * 32 + 16 * (half + 1))
                pe.wait_ge(xgT_a, e)
                pe.wait_ge(xgT_d, e)
                transposes(lambda c: chunks(xg[b], c), xg_turned)

            def layer1(e, s, b, m, q):
                if m == 0:
                    pe.wait_ge(w_in[s], q * 64 + 64)
                    pe.wait_ge(xgT_a, e + 1)
                    pe.wait_ge(xgT_d, e + 1)
                pe.wait_ge(g1_ready, e * 2 + (m - 1) if not isinstance(e, int) or e > 0 else 0)
                for c in range(C6):
                    ins = T.matmul(banks[m][:, 0:P], chunks(w1s[s][:, c, :], m), xgT[b][:, c, :],
                                   start=(c == 0), stop=(c == C6 - 1))
                ins.then_inc(l1_done, 1)

            def layer(w, xin, done):
                for m in range(HC):
                    for c in range(HC):
                        ins = T.matmul(banks[2 + m][:, 0:P], chunks(w[:, c, :], m), xin[:, c, :],
                                       start=(c == 0), stop=(c == HC - 1))
                    ins.then_inc(done, 1)

            def group(q, last):
                for s in range(WSLOTS):
                    e, b = q * WSLOTS + s, s % 2
                    more = not (last and s == WSLOTS - 1)
                    q1, s1 = (q, s + 1) if s < WSLOTS - 1 else (q + 1, 0)
                    if more:
                        turn(e + 1, 1 - b, q1, s1 // 2)
                    pe.wait_ge(g1_ready, e * 2 + 2)
                    pe.wait_ge(z_ready, e * 2)
                    layer(w2s[s], hid[0][b], l2_done)
                    if more:
                        layer1(e + 1, s1, 1 - b, 0, q1)
                    pe.wait_ge(g2_ready, e * 2 + 2)
                    layer(w3s[s], hid[1][b], l3_done)
                    if more:
                        layer1(e + 1, s1, 1 - b, 1, q1)
                    pe.wait_ge(z_ready, e * 2 + 2)
                    pe.wait_ge(ya_ready, e)
                    pe.wait_ge(yd_ready, e)
                    for i, done in enumerate((l4a_done, l4_done)):
                        for c in range(HC):
                            ins = T.matmul(banks[4 + i][:, 0:F // 2], hid[2][b][:, c, :],
                                           wls[s][:, c, i * F // 2:(i + 1) * F // 2],
                                           start=(c == 0), stop=(c == HC - 1))
                        ins.then_inc(done, 1)

            turn(0, 0, 0, 0)
            for m in range(HC):
                layer1(0, 0, 0, m, 0)
            run(pe, NX // WSLOTS, group, first=True)
            pe.wait_ge(flag3_ready, 1)
            with pe.If(pe.value_load(flags[0:1, 2:3]) > 0):
                for i in range(2 * NT):
                    pe.wait_ge(extra_step, XS + 4 * i + 3)
                    T.matmul(banks[0][:, 0:2 * OT], ov_a, ov_b.rearrange("p k n -> p (k n)"),
                             start=(i == 0), stop=(i == 2 * NT - 1)).then_inc(extra_step, 1)
                with pe.Fori(0, OT) as j:
                    n = j * XK + (X0 + 1)
                    pe.wait_ge(extra_step, n + 2)
                    pe.wait_ge(ex_in_x, j * 16 + 16)
                    transposes(lambda c: chunks(xg[0], c), extra_step)
                    pe.wait_ge(extra_step, n + 5)
                    pe.wait_ge(ex_in_w, j * 64 + 64)
                    for m in range(HC):
                        for c in range(C6):
                            ins = T.matmul(banks[m][:, 0:P], chunks(w1s[0][:, c, :], m), xgT[0][:, c, :],
                                           start=(c == 0), stop=(c == C6 - 1))
                    ins.then_inc(extra_step, 1)
                    for k, w in enumerate((w2s[0], w3s[0])):
                        pe.wait_ge(extra_step, n + (8 if k == 0 else 11) + k * 0)
                        for m in range(HC):
                            for c in range(HC):
                                ins = T.matmul(banks[2 + m][:, 0:P], chunks(w[:, c, :], m), hid[k][0][:, c, :],
                                               start=(c == 0), stop=(c == HC - 1))
                        ins.then_inc(extra_step, 1 if k == 0 else 2)
                    pe.wait_ge(extra_step, n + 15)
                    for i in range(2):
                        for c in range(HC):
                            ins = T.matmul(banks[4 + i][:, 0:F // 2], hid[2][0][:, c, :],
                                           wls[0][:, c, i * F // 2:(i + 1) * F // 2],
                                           start=(c == 0), stop=(c == HC - 1))
                    ins.then_inc(extra_step, 1)


_INS = ['x', 'src', 'dst', 'L0_gnn_W_fc', 'L0_gnn_attn_l', 'L0_gnn_attn_r', 'L0_gnn_W_res', 'L0_ffn_gate_w',
        'L0_ffn_W1', 'L0_ffn_b1', 'L0_ffn_W2', 'L0_ffn_b2', 'L0_ffn_W3', 'L0_ffn_b3', 'L0_ffn_Wl', 'L0_ffn_bl']
_DEBUG = False


def kernel(**inputs):
    import numpy as _np
    import concourse.bacc as _bacc
    from concourse import mybir as _mybir
    from concourse.bass_utils import run_bass_kernel_spmd as _run

    nc = _bacc.Bacc("TRN2", target_bir_lowering=False, num_devices=1)
    arrays, args = {}, []
    for name in _INS:
        a = _np.ascontiguousarray(inputs[name])
        arrays[f"in_{name}"] = a
        args.append(nc.dram_tensor(f"in_{name}", a.shape, _mybir.dt.from_np(a.dtype), kind="ExternalInput").ap())
    n, f = inputs['x'].shape
    padded = -(-n // 128) * 128
    out = nc.dram_tensor("out", (n, f), _mybir.dt.float32, kind="ExternalOutput").ap()
    kind = "ExternalOutput" if _DEBUG else "Internal"
    h2 = nc.dram_tensor("h2", (padded, f), _mybir.dt.float32, kind=kind).ap()
    y = nc.dram_tensor("y", (2 * padded, f), _mybir.dt.float32, kind=kind).ap()
    res = nc.dram_tensor("res", (padded, f), _mybir.dt.float32, kind=kind).ap()
    gnn_moe_kernel(nc, *args, out, h2, y, res)
    r = _run(nc, [arrays], core_ids=[0])
    return r.results[0]["out"]
```

```python
from contextlib import ExitStack

import concourse.bass as bass
from concourse import mybir

ALU = mybir.AluOpType
ACT = mybir.ActivationFunctionType
AX = mybir.AxisListType
F32 = mybir.dt.float32
BF16 = mybir.dt.bfloat16
F16 = mybir.dt.float16
I32 = mybir.dt.int32
U32 = mybir.dt.uint32
RMAX = bass.bass_isa.ReduceOp.max

P = 128
SLOPE = 0.2
LN_EPS = 1e-5
GSIZE = 2
WIN = 48
CRING = 8
WSTEP = CRING // GSIZE
WRING = 2
SRING = 4
ACAST = 6
BIAS1 = 4
SIGN0 = 4
SIGNM = 7
NEG = 2
WSLOTS = 4
MAX_RANGE = 60.0
MAX_COUNT = 256.0
FAR = 8192.0


class Chain:

    def __init__(self, eng, sem):
        self.eng, self.sem, self.n = eng, sem, 0

    def link(self, ins):
        ins.then_inc(self.sem, 1)
        self.n = self.n + 1
        self.eng.wait_ge(self.sem, self.n)


def at_col(a, i):
    return a[:, i:i + 1] if isinstance(i, int) else a[:, bass.ds(i, 1)]


def at_mid(a, i):
    return a[:, i] if isinstance(i, int) else a[:, bass.ds(i, 1)].squeeze(1)


def run(eng, n, body, chain=None, links=0, first=False):
    n0 = chain.n if chain else 0
    if first:
        body(0, False)
    with eng.Fori(int(first), n - 1) as q:
        if chain:
            chain.n = n0 + q * links
        body(q, False)
    if chain:
        chain.n = n0 + (n - 1) * links
    body(n - 1, True)


def gnn_moe_kernel(nc, x, src, dst, W_fc, attn_l, attn_r, W_res, gate_w,
                   W1, b1, W2, b2, W3, b3, Wl, bl, out, h2_dram, y_dram, res_dram):
    N, F = x.shape
    H, D = attn_l.shape
    E = src.shape[0]
    NX, _, HID = W1.shape
    NT = -(-N // P)
    NP = NT * P
    LAST = N - (NT - 1) * P
    C6 = F // P
    HC = HID // P
    ET = E // P
    EREM = E - ET * P
    ETP = 160
    ET1 = ETP - P
    NG = ETP // GSIZE
    CW = NP + WIN
    KW = NT * WIN
    D1 = D + 1
    ITS = [(0, NT // 2), (NT // 2, NT)]
    NS = NT - SIGN0
    PART = NT // 2 * P
    MORE = -(-N // WIN)
    OT = 2 * N // P
    assert NT == 10 and F == 768 and H == 12 and D == 64 and NX == 32 and HID == 256

    with ExitStack() as ctx:
        def sb(name, shape, dt=F32):
            return ctx.enter_context(nc.sbuf_tensor(name, shape, dt))

        def sem(name):
            return ctx.enter_context(nc.semaphore(name))

        banks = [ctx.enter_context(nc.psum_tensor(f"bank{i}", [P, 512], F32)) for i in range(6)]
        duo = ctx.enter_context(nc.psum_tensor("duo", [P, 2, 512], F32))

        ft = sb("ft", [P, NT * H * D1])
        xp_mem = sb("xp_mem", [P, 2 * 1950 + 1300])
        c_mem = sb("c_mem", [P, NT * CW])
        cbf_mem = sb("cbf_mem", [P, NT * NP // 2])
        agg = sb("agg", [P, NT * H * D1])
        w_mem = sb("w_mem", [P, 16 * HID])

        ft4 = ft[:, :].rearrange("p (t h e) -> p t h e", t=NT, h=H)
        agg4 = agg[:, :].rearrange("p (t h e) -> p t h e", t=NT, h=H)
        xt = [agg[:, F * i:F * (i + 1)] for i in range(2)]
        ht = [agg[:, F * (2 + i):F * (3 + i)] for i in range(2)]
        hTt = [agg[:, F * (4 + i):F * (5 + i)].rearrange("p (c n) -> p c n", c=C6) for i in range(2)]
        rt = [agg[:, F * (6 + i):F * (7 + i)] for i in range(2)]
        c32 = c_mem[:, :].rearrange("p (t w) -> p t w", t=NT)
        cbf = cbf_mem[:, :].bitcast(BF16).rearrange("p (t n) -> p t n", t=NT)
        oha = xp_mem[:, 0:CRING * P // 2].bitcast(BF16).rearrange("p (r n) -> p r n", r=CRING)
        ohb = xp_mem[:, CRING * P // 2:CRING * P // 2 + CRING * KW // 2].bitcast(BF16)\
            .rearrange("p (r n) -> p r n", r=CRING)
        xp = [xp_mem[:, 1950 * i:1950 * (i + 1)].bitcast(BF16)
              .rearrange("p (t k b e) -> p t k b e", t=NT, k=3, b=2) for i in range(2)]
        x12 = xp_mem[:, 3900:5200].rearrange("p (t b e) -> p t b e", t=NT, b=2)
        cm = c_mem[:, 0:2 * NT * NP // 2].bitcast(BF16)
        mask, nmask = [], []
        off = 0
        for lo, hi in ITS:
            n = NT * (hi - lo) * P
            mask.append(cm[:, off:off + n].rearrange("p (t n) -> p t n", t=NT))
            nmask.append(cm[:, off + n:off + 2 * n].rearrange("p (t n) -> p t n", t=NT))
            off += 2 * n
        base = c_mem[:, 0:NT * F].rearrange("p (t f) -> p t f", t=NT)
        def turned2(s, i):
            return duo[:, i, 0:3 * P] if s == 0 else banks[2 + i][:, 0:3 * P]

        def bias_bank(t, i):
            return banks[(1 + 2 * (t % 3) + i) % 6][:, 0:F // 2]

        wslot = [w_mem[:, :], cbf_mem[:, 0:16 * HID], xp_mem[:, 0:16 * HID],
                 c_mem[:, NT * F:NT * F + 16 * HID]]
        w1s = [w[:, 0:C6 * HID].rearrange("p (c m) -> p c m", c=C6) for w in wslot]
        w2s = [w[:, 6 * HID:8 * HID].rearrange("p (c m) -> p c m", c=HC) for w in wslot]
        w3s = [w[:, 8 * HID:10 * HID].rearrange("p (c m) -> p c m", c=HC) for w in wslot]
        wls = [w[:, 10 * HID:16 * HID].rearrange("p (c m) -> p c m", c=HC) for w in wslot]
        xg = [ft[:, F * i:F * (i + 1)] for i in (0, 1, 8, 9)]
        xgT = [ft[:, F * (2 + i):F * (3 + i)].rearrange("p (c n) -> p c n", c=C6) for i in range(2)]
        ys = [ft[:, F * (4 + i):F * (5 + i)] for i in range(2)]
        hid = [[ft[:, F * 6 + HID * (3 * i + k):F * 6 + HID * (3 * i + k + 1)]
                .rearrange("p (c n) -> p c n", c=HC) for i in range(2)] for k in range(3)]
        YR = 4
        ypair = [agg[:, 2 * F * i:2 * F * (i + 1)] for i in range(YR)]
        xres = [[ft[:, F * (4 + 2 * k + i):F * (5 + 2 * k + i)] for i in range(2)] for k in range(2)]

        def carve(mem, at_float, shape, dt=F32, parts=P):
            n = 1
            for d in shape:
                n *= d
            a = mem[0:parts, at_float:at_float + n]
            if dt != F32:
                a = a.bitcast(dt)
            if len(shape) > 1:
                names = "abcd"[:len(shape)]
                a = a.rearrange(f"p ({' '.join(names)}) -> p {' '.join(names)}",
                                **{c: d for c, d in zip(names[:-1], shape)})
            return a

        o = CRING * (P + KW) // 2
        edges = carve(xp_mem, o, [4, P], I32)
        edges_f = carve(xp_mem, o + 4 * P, [4, P])
        sd_t = carve(xp_mem, o + 8 * P, [2, ETP])
        o += 8 * P + 2 * ETP
        si, jt_i, jp_i = [carve(xp_mem, o + ETP * i, [ETP], I32) for i in range(3)]
        jt_f, dd, pen = [carve(xp_mem, o + ETP * i, [ETP]) for i in range(3, 6)]
        o = 8 * F
        bdn = carve(agg, o, [2, P])
        bd = carve(agg, o + 2 * P, [2, P])
        at = carve(agg, o + 4 * P, [C6, 2 * H])
        bda = carve(agg, o + 4 * P + C6 * 2 * H, [C6, 2 * H])
        pen2 = carve(xp_mem, CRING * (P + KW) // 2 + 4 * P, [ETP])
        o = 8 * F + 4 * P + 2 * C6 * 2 * H
        apart = agg[:, o:o + CRING * P // 2].bitcast(BF16).rearrange("p (k r n) -> p k r n", k=2, r=CRING // 2)
        jneg = carve(agg, o + CRING * P // 2, [ETP])
        gate_n = carve(w_mem, 0, [F], parts=NX)
        bn = carve(w_mem, F, [3, HID], parts=NX)
        o = 16 * HID
        mk = carve(cbf_mem, o, [NT, 2, NX])
        o += NT * 2 * NX
        lg, ex, rk, gm = [carve(cbf_mem, o + NT * NX * i, [NT, NX]) for i in range(4)]
        sla = carve(xp_mem, 16 * HID, [4, P])
        o = 16 * HID + 4 * P
        msum, macc = [carve(xp_mem, o + NT * NX // 2 * i, [NT * NX // 2])
                      .bitcast(BF16).rearrange("p (t n) -> p t n", t=NT) for i in range(2)]
        slb = carve(agg, YR * 2 * F, [NT, 2, 2, NX])
        rkm = carve(agg, YR * 2 * F + NT * 4 * NX, [NT, NX])

        c_in = cbf_mem[:, 3 * NP:4 * NP].rearrange("p (t n) -> p t n", t=NT)
        c_row, none_row, e_row, p_row = [cbf_mem[:, i * NP:(i + 1) * NP] for i in range(4)]
        p_t = cbf_mem[:, 4 * NP:5 * NP].rearrange("p (t n) -> p t n", t=NT)
        ov_a = carve(agg, 0, [P])
        ov_b = carve(agg, P, [2, OT])
        ov_v = carve(agg, 2 * P, [2, OT])
        ov_f = carve(agg, 3 * P, [OT])
        ov_s, ov_g = [carve(agg, 3 * P + 32 * i, [OT], I32) for i in (1, 2)]
        ov_rank_i, ov_hi_i, ov_lo_i = [carve(agg, 4 * P + 128 + 32 * i, [NT, 2], I32) for i in range(3)]
        ov_hi, ov_lo, ov_ge, ov_base = [carve(agg, 4 * P + 224 + 32 * i, [NT, 2]) for i in range(4)]
        ov_n, ov_first, ov_end = [carve(agg, 7 * P + 32 * i, [NX]) for i in range(3)]
        ov_ni = carve(agg, 7 * P + 96, [NX], I32)
        ov_tab = carve(agg, 8 * P, [OT, NX])
        ov_tab2 = carve(agg, 8 * P + OT * NX, [OT, NX])
        ov_ex = carve(agg, 8 * P + 2 * OT * NX, [OT])
        ov_exi = carve(agg, 8 * P + 2 * OT * NX + 32, [OT], I32)
        ov_m = carve(agg, 8 * P + 2 * OT * NX + 64, [NT, NX])
        iota_o = carve(agg, 8 * P + 2 * OT * NX + 64 + NT * NX, [OT])

        ident = sb("ident", [P, P])
        ones_f = sb("ones_f", [P, P])
        ones_b = sb("ones_b", [P, P], BF16)
        before = sb("before", [P, P], BF16)
        iota_p = sb("iota_p", [P, P], F16)
        iota_k = sb("iota_k", [P, KW], F16)
        iota_x = sb("iota_x", [P, NX])
        pair_id = sb("pair_id", [P, NT * 2])
        valid = sb("valid", [P, 1])
        tmin = sb("tmin", [P, 2])
        lo_row = sb("lo_row", [1, ETP])
        lo_min = sb("lo_min", [1, NG])
        lo_int = sb("lo_int", [1, NG], I32)
        key = sb("key", [P, ETP])
        jp_h = sb("jp_h", [P, ETP], F16)
        bns = sb("bns", [P, 2, 6])
        mv = sb("mv", [P, 2])
        ve = sb("ve", [P, 1])
        sd = sb("sd", [P, 1])
        rstd = sb("rstd", [P, 1])
        a12 = sb("a12", [P, NT, 2 * H])
        na1 = sb("na1", [P, NT, H])
        far = sb("far", [P, 1])
        far_all = sb("far_all", [P, 1])
        degree = sb("degree", [P, NT])
        red = sb("red", [P, 3])
        allr = sb("allr", [P, 3])
        flag_f = sb("flag_f", [1, 4])
        flags = sb("flags", [1, 3], I32)
        rank_max = sb("rank_max", [P, 1])
        rank_all = sb("rank_all", [P, 1])
        m_row = sb("m_row", [P, 1])
        n_all = sb("n_all", [P, NX])
        nA = sb("nA", [P, 2])
        sA = sb("sA", [P, NT, H])
        fa = sb("fa", [P, 2, NT, H])
        e12 = sb("e12", [P, 2, NT, H])
        f12 = sb("f12", [P, 2, NT, H])
        a2T = sb("a2T", [H, NP])
        a2m = sb("a2m", [H, NP])
        a2b = sb("a2b", [P, NP])
        gmT = a2b[0:NX, :]
        t2 = sb("t2", [P, SRING, D1])
        rden = sb("rden", [P, NT, H])
        gateT = sb("gateT", [P, C6, NX])
        bT = sb("bT", [P, 3, HC, NX])
        bln = sb("bln", [NX, F])
        mx8 = sb("mx8", [P, NT, 8])
        ix8 = sb("ix8", [P, NT, 8], U32)
        ixf = sb("ixf", [P, NT, 2])
        ex1 = sb("ex1", [P, NT])
        pr = sb("pr", [P, 2, NT])
        psum_pr = sb("psum_pr", [P, NT])
        wk = sb("wk", [P, NT, 2])
        rank = sb("rank", [P, NT, 2])
        slot_v = sb("slot_v", [P, 2, NX])
        slot_f = sb("slot_f", [P, NX])
        slot_s = sb("slot_s", [P, NX], I32)
        slot_g = sb("slot_g", [P, NX], I32)
        gi = [sb(f"gi{i}", [P, 1], I32) for i in range(WSLOTS)]
        so = [sb(f"so{i}", [P, 1], I32) for i in range(2)]

        (const_ready, jneg_ready, apart_ready, pool_chain,
         dve_chain, edges_zeroed, edges_in, gnnw_zeroed, gnnw_in, small_in,
         edges_float, edges_turned, lo_ready, lo_spread, key_ready, oha_ready, ohb_ready,
         window_done, window_added, counts_ready, bd_turned, bd_ready, bda_done, bda_ready,
         var1_ready, sd1_ready, var2_ready, sd2_ready, h_ready, h_turned, hT_ready, ft_done,
         ft_ready, res_copied, red_ready, allr_ready, fa_ready, e_made, e_ready, a2_turned,
         a2T_ready, small_turned, smallT_ready, a2m_ready, a2_spread, a2b_ready, compared,
         mask_ready, x_made, hi_ready, rest_made, mid_ready, xp_ready, sums_done, t2_ready,
         sums_added, x1_ready, h2_ready, h2_turned, h2T_ready, logits_done, logits_read, ex_in,
         ex_lg, ex_made, ex_ready, m_ready, rank_done, gm_ready, gm_turned, gmT_ready, sl_ready,
         slots_done, slots_ready, bias_done, base_ready, xg_zeroed, xg_turned, xgT_a, xgT_d,
         l1_done, g1_ready, l2_done, g2_ready, l3_done, z_ready, l4a_done, l4_done, ya_ready,
         yd_ready, gathers_begun, scatters_begun, neg_ready, signs_begun, signed, multiplied, cut,
         ft_free, rden_ready, scaled, res_added, maxed, maxed_index, counts_added, counts_zeroed,
         const2_ready, far_ready, far_all_ready, flag1_ready, more_step, flag2_ready, wide_step,
         attention_done, rank_max_ready, rank_all_ready, flag3_ready, extra_step, ex_in_w, ex_in_x,
         ex_out, sum_ready, out_done) = [sem(n) for n in (
             "const_ready jneg_ready apart_ready pool_chain "
             "dve_chain edges_zeroed edges_in gnnw_zeroed gnnw_in small_in "
             "edges_float edges_turned lo_ready lo_spread key_ready oha_ready ohb_ready window_done "
             "window_added counts_ready bd_turned bd_ready bda_done bda_ready var1_ready sd1_ready "
             "var2_ready sd2_ready h_ready h_turned hT_ready ft_done ft_ready res_copied red_ready "
             "allr_ready fa_ready e_made e_ready a2_turned a2T_ready small_turned smallT_ready a2m_ready "
             "a2_spread a2b_ready compared mask_ready x_made hi_ready rest_made mid_ready xp_ready "
             "sums_done t2_ready sums_added x1_ready h2_ready h2_turned h2T_ready logits_done "
             "logits_read ex_in ex_lg ex_made ex_ready m_ready rank_done gm_ready gm_turned gmT_ready "
             "sl_ready slots_done slots_ready bias_done base_ready xg_zeroed xg_turned xgT_a xgT_d "
             "l1_done g1_ready l2_done g2_ready l3_done z_ready l4a_done l4_done ya_ready yd_ready "
             "gathers_begun scatters_begun neg_ready signs_begun signed multiplied cut ft_free "
             "rden_ready scaled res_added maxed maxed_index counts_added counts_zeroed const2_ready "
             "far_ready far_all_ready flag1_ready more_step flag2_ready wide_step attention_done "
             "rank_max_ready rank_all_ready flag3_ready extra_step ex_in_w ex_in_x ex_out sum_ready "
             "out_done").split()]
        x_in = [sem(f"x_in{i}") for i in range(2)]
        res_out = [sem(f"res_out{i}") for i in range(2)]
        xr_in = [sem(f"xr_in{i}") for i in range(2)]
        h2_out = [sem(f"h2_out{i}") for i in range(2)]
        w_in = [sem(f"w_in{i}") for i in range(WSLOTS)]
        xg_in = [sem(f"xg_in{i}") for i in range(WSLOTS)]
        y_out = [sem(f"y_out{i}") for i in range(2)]
        ypair_in = [sem(f"ypair_in{i}") for i in range(YR)]

        MK = 8 + 5 * NG
        WH = 17
        W0, WT = 4, 6 + WH * H
        XS = 58
        X0, XK = XS + 4 * 2 * NT + 5, 20

        block = ctx.enter_context(nc.Block())

        def rows(t):
            return LAST if t == NT - 1 else P

        def chunks(a, c):
            n = a.shape[-1] // P
            return a.rearrange("p (q c) -> p c q", c=n)[:, c, :]


        @block.sync
        def _(sp):
            sp.wait_ge(edges_zeroed, 2)
            for k, a in enumerate((src, dst)):
                sp.dma_start(edges[:, k, :], a[0:P * P].rearrange("(t e) -> t e", e=P)).then_inc(edges_in, 16)
                sp.dma_start(edges[0:ET - P, 2 + k, :],
                             a[P * P:ET * P].rearrange("(t e) -> t e", e=P)).then_inc(edges_in, 16)
                sp.dma_start(edges[ET - P:ET - P + 1, 2 + k, 0:EREM],
                             a[ET * P:E].rearrange("(t e) -> t e", t=1)).then_inc(edges_in, 16)
            sp.wait_ge(gnnw_zeroed, 2)
            for k, a in enumerate((W_fc, W_res)):
                for b in range(2):
                    sp.dma_start(bdn[D * b:D * b + D, k, D * b:D * b + D], a).then_inc(gnnw_in, 16)
            with nc.allow_non_contiguous_dma(reason="attention vectors as columns"):
                for k, a in enumerate((attn_l, attn_r)):
                    for b in range(2):
                        sp.dma_start(at[D * b:D * b + D].rearrange("p c n -> p (c n)")
                                     [:, k * H + b:C6 * 2 * H:2 * H + 2],
                                     a.rearrange("(c b) e -> b e c", b=2)[b]).then_inc(gnnw_in, 16)
            for t in range(2):
                sp.dma_start(xt[t], x[t * P:(t + 1) * P, :]).then_inc(x_in[t], 16)
            sp.dma_start(gate_n[:, :], gate_w).then_inc(small_in, 16)
            for k, a in enumerate((b1, b2, b3)):
                sp.dma_start(bn[:, k, :], a).then_inc(small_in, 16)
            sp.dma_start(bln[:, :], bl).then_inc(small_in, 16)
            for t in range(2, NT + 3):
                if t < NT:
                    sp.wait_ge(h_ready, t - 1)
                    sp.dma_start(xt[t % 2][0:rows(t), :], x[t * P:t * P + rows(t), :]).then_inc(x_in[t % 2], 16)
                if t >= 3:
                    u = t - 3
                    sp.wait_ge(res_copied, 3 * (u + 1))
                    sp.dma_start(res_dram[u * P:(u + 1) * P, :], rt[u % 2]).then_inc(res_out[u % 2], 16)

            def load_expert(e, s):
                for tile, w in ((w1s, W1), (w2s, W2), (w3s, W3), (wls, Wl)):
                    w_e = w[e] if isinstance(e, int) else w[bass.ds(e, 1), :, :].squeeze(0)
                    sp.dma_start(tile[s].rearrange("p c m -> p (c m)"),
                                 w_e.rearrange("(p c) m -> p (c m)", p=P)).then_inc(w_in[s], 16)

            sp.wait_ge(smallT_ready, 2)
            load_expert(0, 0)
            for i in range(2):
                sp.wait_ge(res_out[i], 16 * (NT // 2))
            sp.wait_ge(ft_free, 1)
            for t in range(NT + 1):
                if t == 2:
                    sp.wait_ge(attention_done, 1)
                if t >= 2:
                    sp.wait_ge(x1_ready, t - 1)
                if t < NT:
                    sp.dma_start(xres[0][t % 2][0:rows(t), :], x[t * P:t * P + rows(t), :])\
                        .then_inc(xr_in[t % 2], 16)
                    sp.dma_start(xres[1][t % 2], res_dram[t * P:(t + 1) * P, :]).then_inc(xr_in[t % 2], 16)
                if t >= 2:
                    sp.wait_ge(h2_ready, t - 1)
                    sp.dma_start(h2_dram[(t - 2) * P:(t - 1) * P, :], xg[t % 2]).then_inc(h2_out[t % 2], 16)
            sp.wait_ge(h2_ready, NT)
            sp.dma_start(h2_dram[(NT - 1) * P:NT * P, :], xg[1]).then_inc(h2_out[1], 16)
            for s in range(1, WSLOTS):
                load_expert(s, s)
            with sp.Fori(1, NX // WSLOTS) as q:
                for s in range(WSLOTS):
                    sp.wait_ge(l4_done, q * WSLOTS + (s + 1 - WSLOTS))
                    load_expert(q * WSLOTS + s, s)
            sp.wait_ge(flag3_ready, 1)
            with sp.If(sp.value_load(flags[0:1, 2:3]) > 0):
                with sp.Fori(0, OT) as j:
                    sp.wait_ge(extra_step, j * XK + (X0 + 1))
                    e = sp.snap(sp.value_load(at_col(ov_exi[0:1, :], j)), min_val=0, max_val=NX - 1)
                    for tile, w in ((w1s, W1), (w2s, W2), (w3s, W3), (wls, Wl)):
                        sp.dma_start(tile[0].rearrange("p c m -> p (c m)"),
                                     w[bass.ds(e, 1), :, :].squeeze(0)
                                     .rearrange("(p c) m -> p (c m)", p=P)).then_inc(ex_in_w, 16)
                sp.wait_ge(extra_step, X0 + OT * XK + 1)
            for i in range(2):
                sp.wait_ge(y_out[i], 16 * (NX // 2))
            for t in range(NT + YR - 1):
                if t < NT:
                    if t >= YR:
                        sp.wait_ge(sum_ready, t - YR + 1)
                    sp.dma_start(ypair[t % YR][0:rows(t), :],
                                 y_dram[2 * t * P:2 * (t * P + rows(t)), :]
                                 .rearrange("(p k) f -> p (k f)", k=2)).then_inc(ypair_in[t % YR], 16)
                u = t - (YR - 1)
                if u >= 0:
                    sp.wait_ge(sum_ready, u + 1)
                    sp.dma_start(out[u * P:u * P + rows(u), :], base[0:rows(u), u, :]).then_inc(out_done, 16)
            sp.wait_ge(out_done, 16 * NT)

        @block.gpsimd
        def _(pool):
            g = nc.gpsimd
            ch = Chain(pool, pool_chain)
            pool.sem_inc(xp_ready, 1)
            g.memset(edges[:, 2, :], 16000).then_inc(edges_zeroed, 1)
            g.memset(edges[:, 3, :], N - 1).then_inc(edges_zeroed, 1)
            g.memset(bdn[:, :, :], 0.0).then_inc(gnnw_zeroed, 1)
            g.memset(at[:, :, :], 0.0).then_inc(gnnw_zeroed, 1)
            ch.link(g.memset(ident[:, :], 0.0))
            ch.link(g.affine_select(out=ident[:, :], in_=ident[:, :], compare_op=ALU.not_equal, fill=1.0,
                                    base=0, pattern=[[-1, P]], channel_multiplier=1))
            ch.link(g.memset(ones_f[:, :], 1.0))
            for tile, pat in ((iota_p, [[1, P]]), (iota_k, [[1, KW]])):
                ch.link(g.iota(tile[:, :], pattern=pat, base=0, channel_multiplier=0,
                               allow_small_or_imprecise_dtypes=True))
            pool.sem_inc(const_ready, 1)
            g.memset(c_mem[:, :], 0.0).then_inc(counts_zeroed, 1)
            ch.link(g.memset(ones_b[:, :], 1.0))
            ch.link(g.affine_select(out=before[:, :], in_=ones_b[:, :], compare_op=ALU.is_ge, fill=0.0,
                                    base=-1, pattern=[[1, P]], channel_multiplier=-1))
            for tile, pat in ((iota_x, [[1, NX]]),):
                ch.link(g.iota(tile[:, :], pattern=pat, base=0, channel_multiplier=0,
                               allow_small_or_imprecise_dtypes=True))
            ch.link(g.iota(pair_id[:, :], pattern=[[2 * P, NT], [1, 2]], base=1, channel_multiplier=2,
                           allow_small_or_imprecise_dtypes=True))
            ch.link(g.affine_select(out=valid[:, :], in_=ones_f[:, 0:1], compare_op=ALU.is_ge, fill=0.0,
                                    base=LAST - 1, pattern=[[0, 1]], channel_multiplier=-1))
            ch.link(g.memset(ft4[:, :, :, D:D1].rearrange("p t h e -> p (t h) e"), 1.0))
            pool.sem_inc(const2_ready, 1)

            pool.wait_ge(far_ready, 1)
            g.partition_all_reduce(far_all[:, :], far[:, :], P, RMAX).then_inc(far_all_ready, 1)
            pool.wait_ge(red_ready, 2)
            g.partition_all_reduce(allr[:, 0:2], red[:, 0:2], P, RMAX).then_inc(allr_ready, 1)

            pool.wait_ge(e_ready, 1)
            pool.wait_ge(ft_ready, 2 * NT)

            def parts(h, s):
                pool.wait_ge(xp_ready, h + 1)
                for b in range(2):
                    g.tensor_tensor(x12[:, :, b, :], at_mid(ft4.rearrange("p t h e -> p h t e"), h),
                                    at_mid(e12[:, b].rearrange("p t h -> p h t"), h).unsqueeze(2)
                                    .broadcast_to([P, NT, D1]), ALU.mult).then_inc(x_made, 1)
                pool.wait_ge(hi_ready, h + 1)
                g.tensor_tensor(x12, x12, xp[s][:, :, 0], ALU.subtract).then_inc(rest_made, 1)
                pool.wait_ge(mid_ready, h + 1)
                g.tensor_tensor(xp[s][:, :, 2], x12, xp[s][:, :, 1], ALU.subtract).then_inc(xp_ready, 1)

            parts(0, 0)
            pool.wait_ge(red_ready, 3)
            g.partition_all_reduce(allr[:, 2:3], red[:, 2:3], P, RMAX).then_inc(allr_ready, 1)
            pool.wait_ge(flag2_ready, 1)
            with pool.If(pool.value_load(flags[0:1, 1:2]) < 1):
                parts(1, 1)
                with pool.Fori(1, H // 2) as hh:
                    for s in range(2):
                        parts(hh * 2 + s, s)
                pool.wait_ge(xp_ready, H + 1)
            with pool.Else():
                pool.wait_ge(wide_step, 1 + W0 + NT * WT)
            pool.sem_inc(ft_free, 1)

            pool.wait_ge(rden_ready, 1)

            for t in range(NT):
                g.tensor_tensor(base[:, t].rearrange("p (h e) -> p h e", h=H), agg4[:, t, :, 0:D],
                                rden[:, t].unsqueeze(2).broadcast_to([P, H, D]), ALU.mult).then_inc(scaled, 1)
                pool.wait_ge(scaled, t + 1)
                pool.wait_ge(xr_in[t % 2], t // 2 * 32 + 32)
                g.tensor_tensor(base[:, t], base[:, t], xres[1][t % 2], ALU.add).then_inc(res_added, 1)

            for i in range(2):
                pool.wait_ge(h2_out[i], 16 * (NT // 2))
            pool.wait_ge(h2_turned, 2 + NT)
            for i in range(WSLOTS):
                g.memset(xg[i], 0.0).then_inc(xg_zeroed, 1)
            pool.wait_ge(xg_zeroed, WSLOTS)
            pool.wait_ge(rank_max_ready, 1)
            g.partition_all_reduce(rank_all[:, :], rank_max[:, :], P, RMAX).then_inc(rank_all_ready, 1)
            pool.wait_ge(slots_ready, 1)

            token_bound = pool.to_reg(NP - 1)
            row_bound = pool.to_reg(2 * NP - 1)

            def gather(e, b):
                ch.link(g.tensor_copy(gi[b][:, :], at_col(slot_g, e)))
                pool.sem_inc(gathers_begun, 1)
                g.indirect_dma_start(xg[b], None, h2_dram, bass.IndirectOffsetOnAxis(gi[b][:, 0:1], 0),
                                     bounds_check=token_bound, oob_is_err=False).then_inc(xg_in[b], 16)

            def scatter(e, b):
                ch.link(g.tensor_copy(so[b][:, :], at_col(slot_s, e)))
                pool.wait_ge(ya_ready, e + 1)
                pool.wait_ge(yd_ready, e + 1)
                pool.sem_inc(scatters_begun, 1)
                g.indirect_dma_start(y_dram, bass.IndirectOffsetOnAxis(so[b][:, 0:1], 0), ys[b], None,
                                     bounds_check=row_bound, oob_is_err=False).then_inc(y_out[b], 16)

            for s in range(WSLOTS):
                gather(s, s)

            def group(q, last):
                for s in range(WSLOTS):
                    e = q * WSLOTS + s
                    if not last:
                        pool.wait_ge(xg_turned, e + 1)
                        gather(e + WSLOTS, s)
                    pool.wait_ge(y_out[s % 2], q * 32 + 16 * (s // 2))
                    scatter(e, s % 2)

            run(pool, NX // WSLOTS, group, ch, 2 * WSLOTS, first=True)
            pool.wait_ge(flag3_ready, 1)
            with pool.If(pool.value_load(flags[0:1, 2:3]) > 0):
                g.iota(iota_o, pattern=[[1, OT]], base=0, channel_multiplier=0,
                       allow_small_or_imprecise_dtypes=True).then_inc(extra_step, 1)
                pool.wait_ge(y_out[0], NX // 2 * 16)
                with pool.Fori(0, OT) as j:
                    pool.wait_ge(extra_step, j * XK + (X0 + 1))
                    g.tensor_copy(gi[0][:, :], at_col(ov_g, j)).then_inc(extra_step, 1)
                    pool.wait_ge(extra_step, j * XK + (X0 + 2))
                    g.tensor_copy(so[0][:, :], at_col(ov_s, j)).then_inc(extra_step, 1)
                    pool.wait_ge(extra_step, j * XK + (X0 + 3))
                    pool.sem_inc(gathers_begun, 1)
                    g.indirect_dma_start(xg[0], None, h2_dram, bass.IndirectOffsetOnAxis(gi[0][:, 0:1], 0),
                                         bounds_check=token_bound, oob_is_err=False).then_inc(ex_in_x, 16)
                    pool.wait_ge(extra_step, j * XK + (X0 + XK - 1))
                    pool.sem_inc(scatters_begun, 1)
                    g.indirect_dma_start(y_dram, bass.IndirectOffsetOnAxis(so[0][:, 0:1], 0), ys[0], None,
                                         bounds_check=row_bound, oob_is_err=False).then_inc(ex_out, 16)
                    pool.wait_ge(ex_out, j * 16 + 16)
                    pool.sem_inc(extra_step, 2)

        @block.vector
        def _(dve):
            v = nc.vector
            ch = Chain(dve, dve_chain)
            link = ch.link
            dve.sem_inc(window_added, WRING)
            dve.sem_inc(compared, 2 * SIGN0)
            dve.sem_inc(sums_added, SRING)
            dve.wait_ge(edges_in, 16 * 6)
            v.tensor_copy(edges_f[:, 0:2, :], edges[:, 0:2, :]).then_inc(edges_float, 1)
            v.tensor_copy(edges_f[0:ET1, 2:4, :], edges[0:ET1, 2:4, :]).then_inc(edges_float, 1)
            dve.wait_ge(edges_float, 2)
            v.tensor_reduce(tmin[:, 0:1], edges_f[:, 1, :], AX.X, ALU.min).then_inc(edges_float, 1)
            v.tensor_reduce(tmin[0:ET1, 1:2], edges_f[0:ET1, 3, :], AX.X, ALU.min).then_inc(edges_float, 1)
            dve.wait_ge(edges_turned, 1)
            link(v.tensor_copy(lo_row[0:1, :], banks[1][0:1, 0:ETP]))
            link(v.tensor_reduce(lo_min[0:1, :], lo_row[0:1, :].rearrange("p (g k) -> p g k", k=GSIZE),
                                 AX.X, ALU.min))
            v.tensor_copy(lo_int[0:1, :], lo_min[0:1, :]).then_inc(lo_ready, 1)
            link(v.tensor_copy(sd_t[:, :, :], banks[0][:, 0:2 * ETP].rearrange("p (k t) -> p k t", k=2)))
            link(v.tensor_copy(si[:, :], sd_t[:, 0, :]))
            link(v.tensor_single_scalar(jt_i[:, :], si[:, :], 7, ALU.logical_shift_right))
            link(v.tensor_single_scalar(jp_i[:, :], si[:, :], P - 1, ALU.bitwise_and))
            link(v.tensor_copy(jt_f[:, :], jt_i[:, :]))
            link(v.tensor_copy(jp_h[:, :], jp_i[:, :]))
            v.tensor_scalar(jneg, jp_h[:, :], -1.0, None, ALU.mult).then_inc(jneg_ready, 1)
            dve.wait_ge(lo_spread, 1)
            link(v.tensor_tensor(dd[:, :].rearrange("p (g k) -> p g k", k=GSIZE),
                                 sd_t[:, 1, :].rearrange("p (g k) -> p g k", k=GSIZE),
                                 banks[2][:, 0:NG].unsqueeze(2).broadcast_to([P, NG, GSIZE]), ALU.subtract))
            link(v.tensor_scalar(pen[:, :], dd[:, :], float(WIN), FAR, ALU.is_ge, ALU.mult))
            link(v.scalar_tensor_tensor(key[:, :], jt_f[:, :], float(WIN), dd[:, :], ALU.mult, ALU.add))
            v.tensor_reduce(far[:, :], pen[:, :], AX.X, ALU.max).then_inc(far_ready, 1)
            v.tensor_tensor(key[:, :], key[:, :], pen[:, :], ALU.add).then_inc(key_ready, 1)
            dve.wait_ge(bd_turned, 1)
            v.tensor_copy(bd[:, :, :], banks[3][:, 0:2 * P].rearrange("p (k n) -> p k n", k=2)).then_inc(bd_ready, 1)
            dve.wait_ge(bda_done, 1)
            v.tensor_copy(bda[:, :, :], banks[4][:, 0:C6 * 2 * H].rearrange("p (c n) -> p c n", c=C6))\
                .then_inc(bda_ready, 1)
            dve.wait_ge(key_ready, 1)
            dve.wait_ge(lo_ready, 1)
            dve.wait_ge(const_ready, 1)

            def one_hot_columns(q, part, i):
                r = part * CRING // 2 + i
                if i == 0:
                    dve.wait_ge(window_done, q * WSTEP + (part + 1) * (WSTEP // 2))
                v.tensor_scalar(ohb[:, r, :], iota_k[:, :], at_col(key, q * CRING + r), None,
                                ALU.is_equal).then_inc(ohb_ready, 1)

            def add_window(q, part, i):
                w = part * WSTEP // 2 + i
                gq = q * WSTEP + w
                lo = dve.value_load(at_col(lo_int[0:1, :], gq), min_val=0, max_val=N - 1)
                dve.wait_ge(window_done, gq + (WSTEP + 1))
                dve.wait_ge(window_added, gq + WRING)
                v.tensor_tensor(c32[:, :, bass.ds(lo, WIN)], c32[:, :, bass.ds(lo, WIN)],
                                banks[w % WRING][:, 0:KW].rearrange("p (t n) -> p t n", t=NT), ALU.add)\
                    .then_inc(window_added, 1)

            def windows(q, last):
                for part in range(2):
                    q1, p1 = (q, 1) if part == 0 else (q + 1, 0)
                    more = not (last and part == 1)
                    if more:
                        one_hot_columns(q1, p1, 0)
                    add_window(q, part, 0)
                    if more:
                        one_hot_columns(q1, p1, 1)
                        one_hot_columns(q1, p1, 2)
                    add_window(q, part, 1)
                    if more:
                        one_hot_columns(q1, p1, 3)

            def norm(t, xin, hout, var_ready, sd_ready, done, meanwhile=None):
                for i in range(2):
                    link(v.bn_stats(bns[:, i, :], xin[:, i * F // 2:(i + 1) * F // 2]))
                dve.wait_ge(done, t)
                link(v.bn_aggr(mv[:, :], bns[:, :, :]))
                v.tensor_scalar(ve[:, :], mv[:, 1:2], LN_EPS, None, ALU.add).then_inc(var_ready, 1)
                if meanwhile:
                    meanwhile()
                dve.wait_ge(sd_ready, t + 1)
                link(v.reciprocal(rstd[:, :], sd[:, :]))
                v.tensor_scalar(hout, xin, mv[:, 0:1], rstd[:, 0:1], ALU.subtract, ALU.mult).then_inc(done, 1)

            def norm1(t, s, q):
                dve.wait_ge(x_in[s], q * 16 + 16)
                dve.wait_ge(h_turned, t + 1)
                norm(t, xt[s], ht[s], var1_ready, sd1_ready, h_ready)

            def copy_sums(t):
                s = t % 2
                if t >= 2:
                    dve.wait_ge(res_out[s], t // 2 * 16)
                dve.wait_ge(ft_done, t * 2 + 2)
                v.tensor_copy(rt[s][:, 0:512], banks[4][:, :]).then_inc(res_copied, 1)
                v.tensor_copy(rt[s][:, 512:F], banks[5][:, 0:F - 512]).then_inc(res_copied, 1)
                v.tensor_copy(a12[:, t], banks[5][:, 256:256 + 2 * H]).then_inc(res_copied, 1)

            for i in range(CRING // 2):
                one_hot_columns(0, 0, i)
            norm1(0, 0, 0)
            dve.wait_ge(counts_zeroed, 1)
            QT = ETP // CRING // NT
            assert QT == 2 and QT * NT * CRING == ETP
            for t in range(NT):
                with dve.Fori(QT * t, QT * t + 1) as q:
                    windows(q, False)
                if t >= 1:
                    copy_sums(t - 1)
                if t < NT - 1:
                    norm1(t + 1, (t + 1) % 2, (t + 1) // 2)
                if t < NT - 1:
                    with dve.Fori(QT * t + 1, QT * t + 2) as q:
                        windows(q, False)
                else:
                    windows(QT * t + 1, True)
            copy_sums(NT - 1)
            dve.wait_ge(window_added, NG + WRING)
            dve.wait_ge(far_all_ready, 1)
            v.tensor_copy(flags[0:1, 0:1], far_all[0:1, :]).then_inc(flag1_ready, 1)
            dve.wait_ge(flag1_ready, 1)

            with dve.If(dve.value_load(flags[0:1, 0:1]) > 0):
                with dve.Fori(0, MORE) as p_:
                    n = p_ * MK
                    for i, make in enumerate((
                            lambda: v.tensor_scalar(dd, dd, float(WIN), None, ALU.subtract),
                            lambda: v.tensor_scalar(lo_min[0:1, :], lo_min[0:1, :], float(WIN), float(N),
                                                    ALU.add, ALU.min),
                            lambda: v.tensor_copy(lo_int[0:1, :], lo_min[0:1, :]),
                            lambda: v.tensor_scalar(pen, dd, float(WIN), FAR, ALU.is_ge, ALU.mult),
                            lambda: v.tensor_scalar(pen2, dd, 0.0, FAR, ALU.is_lt, ALU.mult),
                            lambda: v.scalar_tensor_tensor(key[:, :], jt_f, float(WIN), dd, ALU.mult, ALU.add),
                            lambda: v.tensor_tensor(pen, pen, pen2, ALU.add),
                            lambda: v.tensor_tensor(key[:, :], key[:, :], pen, ALU.add))):
                        dve.wait_ge(more_step, n + (i + 1))
                        make().then_inc(more_step, 1)
                    with dve.Fori(0, NG) as gq:
                        m = n + gq * 5
                        dve.wait_ge(more_step, m + 9)
                        v.tensor_tensor(oha[:, 0:GSIZE, :], iota_p[:, :].unsqueeze(1).broadcast_to([P, GSIZE, P]),
                                        jp_h[:, bass.ds(gq * GSIZE, GSIZE)].unsqueeze(2)
                                        .broadcast_to([P, GSIZE, P]), ALU.is_equal).then_inc(more_step, 1)
                        for r in range(GSIZE):
                            v.tensor_scalar(ohb[:, r, :], iota_k[:, :], at_col(key, gq * GSIZE + r), None,
                                            ALU.is_equal).then_inc(more_step, 1)
                        lo = dve.value_load(at_col(lo_int[0:1, :], gq), min_val=0, max_val=N)
                        dve.wait_ge(more_step, m + 13)
                        v.tensor_tensor(c32[:, :, bass.ds(lo, WIN)], c32[:, :, bass.ds(lo, WIN)],
                                        banks[0][:, 0:KW].rearrange("p (t n) -> p t n", t=NT), ALU.add)\
                            .then_inc(more_step, 1)
                dve.wait_ge(more_step, 1 + MORE * MK)
            dve.sem_inc(counts_added, 1)

            dve.wait_ge(res_copied, 3 * NT)
            v.tensor_reduce(red[:, 0:1], a12[:, :, 0:H], AX.XY, ALU.max).then_inc(red_ready, 1)
            link(v.tensor_scalar(na1[:, :, :], a12[:, :, 0:H], -1.0, None, ALU.mult))
            v.tensor_reduce(red[:, 1:2], na1[:, :, :], AX.XY, ALU.max).then_inc(red_ready, 1)
            dve.wait_ge(allr_ready, 1)
            link(v.tensor_scalar(nA[:, 0:1], allr[:, 0:1], -1.0, None, ALU.mult))
            link(v.tensor_scalar(nA[:, 1:2], allr[:, 0:1], -SLOPE, None, ALU.mult))
            link(v.tensor_scalar(sA[:, :, :], a12[:, :, H:2 * H], allr[:, 0:1], None, ALU.add))
            link(v.tensor_scalar(fa[:, 0], sA[:, :, :], 1.0 - SLOPE, 0.0, ALU.mult, ALU.min))
            v.tensor_scalar(fa[:, 1], sA[:, :, :], SLOPE - 1.0, 0.0, ALU.mult, ALU.min).then_inc(fa_ready, 1)
            dve.wait_ge(small_turned, 1)
            v.tensor_copy(gateT[:, :, :], banks[3][:, 0:C6 * NX].rearrange("p (c n) -> p c n", c=C6))\
                .then_inc(smallT_ready, 1)
            v.tensor_copy(bT[:, :, :, :].rearrange("p k c n -> p (k c n)"),
                          banks[3][:, C6 * NX:C6 * NX + 3 * HC * NX]).then_inc(smallT_ready, 1)
            v.tensor_reduce(degree[:, ACAST:NT], c32[:, ACAST:NT, 0:NP], AX.X, ALU.add)\
                .then_inc(counts_ready, NT - ACAST)
            v.tensor_copy(cbf[:, ACAST:NT, :], c32[:, ACAST:NT, 0:NP]).then_inc(counts_ready, 1)
            dve.wait_ge(counts_ready, NT + 1)
            v.tensor_reduce(red[:, 2:3], degree[:, :], AX.X, ALU.max).then_inc(red_ready, 1)
            dve.wait_ge(allr_ready, 2)
            link(v.tensor_tensor(flag_f[:, 0:1], allr[0:1, 0:1], allr[0:1, 1:2], ALU.add))
            link(v.tensor_scalar(flag_f[:, 1:2], flag_f[:, 0:1], MAX_RANGE, None, ALU.is_gt))
            link(v.tensor_scalar(flag_f[:, 2:3], allr[0:1, 2:3], MAX_COUNT, None, ALU.is_gt))
            link(v.tensor_tensor(flag_f[:, 3:4], flag_f[:, 1:2], flag_f[:, 2:3], ALU.max))
            v.tensor_copy(flags[0:1, 1:2], flag_f[:, 3:4]).then_inc(flag2_ready, 1)
            dve.wait_ge(flag2_ready, 1)
            dve.wait_ge(e_ready, 1)
            for i in range(2):
                dve.wait_ge(res_out[i], 16 * (NT // 2))

            def masks(h, i, add):
                lo, hi = ITS[i]
                dve.wait_ge(a2b_ready, h * 4 + (2 if i == 0 else 4))
                dve.wait_ge(sums_done, h * NT + (ITS[0][1] if i == 0 else NT))
                for jt in range(SIGN0):
                    v.scalar_tensor_tensor(mask[i][:, jt, :], a2b[:, lo * P:hi * P], at_col(na1[:, jt, :], h),
                                           cbf[:, jt, lo * P:hi * P], ALU.is_ge, ALU.mult).then_inc(compared, 1)
                n = (h * 2 + i) * 2
                for b, (j0, j1) in enumerate(((SIGN0, SIGNM), (SIGNM, NT))):
                    dve.wait_ge(signed, h * (2 * NS) + (2 * NS + i * NS + j1 - SIGN0))
                    v.tensor_tensor(mask[i][:, j0:j1], mask[i][:, j0:j1], cbf[:, j0:j1, lo * P:hi * P],
                                    ALU.mult).then_inc(multiplied, 1)
                    if b == 1:
                        add(0)
                        add(1)
                    dve.wait_ge(multiplied, n + (b + 1))
                    v.tensor_scalar(mask[i][:, j0:j1], mask[i][:, j0:j1], 0.0, None, ALU.max).then_inc(cut, 1)
                dve.wait_ge(compared, h * (2 * SIGN0) + (2 * SIGN0 + (i + 1) * SIGN0))
                dve.wait_ge(cut, n + 2)
                v.tensor_tensor(nmask[i][:, NEG:NT], mask[i][:, NEG:NT], cbf[:, NEG:NT, lo * P:hi * P],
                                ALU.subtract).then_inc(mask_ready, 1)
                for t in range(2, 5):
                    add(t)

            def add_sum(h, s, t):
                r = (s * NT + t) % SRING
                dve.wait_ge(t2_ready, h * NT + (t + 1))
                v.scalar_tensor_tensor(at_mid(agg4[:, t], h), banks[r][:, 0:D1], at_col(f12[:, 0, t, :], h),
                                       t2[:, r, :], ALU.mult, ALU.subtract).then_inc(sums_added, 1)

            def heads(hh, last):
                for s in range(2):
                    h = hh * 2 + s
                    masks(h, 1, lambda t: add_sum(h, s, t))
                    if last and s == 1:
                        for t in range(NT // 2, NT):
                            add_sum(h, s, t)
                    else:
                        masks(h + 1, 0, lambda t: add_sum(h, s, NT // 2 + t))

            wide = dve.value_load(flags[0:1, 1:2])
            with dve.If(wide < 1):
                for i, (lo, hi) in enumerate(ITS):
                    v.tensor_scalar(nmask[i][:, 0:NEG], cbf[:, 0:NEG, lo * P:hi * P], -1.0, None, ALU.mult)\
                        .then_inc(neg_ready, 1)
                masks(0, 0, lambda jt: None)
                run(dve, H // 2, heads)
                dve.wait_ge(sums_added, SRING + H * NT)
            with dve.Else():
                with dve.Fori(0, NT) as t:
                    n = t * WT + W0
                    dve.wait_ge(wide_step, n + 1)
                    v.tensor_copy(c_in, c32[:, :, bass.ds(t * P, P)]).then_inc(wide_step, 1)
                    dve.wait_ge(wide_step, n + 3)
                    for i in range(3):
                        m = min(512, NP - 512 * i)
                        v.tensor_copy(c_row[:, 512 * i:512 * i + m], banks[i][:, 0:m]).then_inc(wide_step, 1)
                    dve.wait_ge(wide_step, n + 6)
                    v.tensor_scalar(none_row, c_row, 0.0, -3e38, ALU.is_equal, ALU.mult).then_inc(wide_step, 1)
                    with dve.Fori(0, H) as h:
                        c = n + h * WH + 7
                        dve.wait_ge(wide_step, c + 2)
                        for i in range(3):
                            m = min(512, NP - 512 * i)
                            v.tensor_scalar(e_row[:, 512 * i:512 * i + m], banks[3 + i][:, 0:m],
                                            a12[:, bass.ds(t, 1), bass.ds(h + H, 1)].squeeze(1), None, ALU.add)\
                                .then_inc(wide_step, 1)
                        dve.wait_ge(wide_step, c + 5)
                        v.scalar_tensor_tensor(e_row, e_row, SLOPE, e_row, ALU.mult, ALU.max)\
                            .then_inc(wide_step, 1)
                        dve.wait_ge(wide_step, c + 6)
                        v.tensor_tensor(p_row, e_row, none_row, ALU.add).then_inc(wide_step, 1)
                        dve.wait_ge(wide_step, c + 7)
                        v.tensor_reduce(m_row[:, :], p_row, AX.X, ALU.max).then_inc(wide_step, 1)
                        dve.wait_ge(wide_step, c + 8)
                        v.tensor_scalar(e_row, e_row, m_row[:, 0:1], 0.0, ALU.subtract, ALU.min)\
                            .then_inc(wide_step, 1)
                        dve.wait_ge(wide_step, c + 10)
                        v.tensor_tensor(p_row, e_row, c_row, ALU.mult).then_inc(wide_step, 1)
                        dve.wait_ge(wide_step, c + 12)
                        for i in range(3):
                            m = min(4, NT - 4 * i)
                            v.tensor_copy(p_t[:, 4 * i:4 * i + m, :],
                                          banks[i][:, 0:m * P].rearrange("p (t n) -> p t n", t=m))\
                                .then_inc(wide_step, 1)
                        dve.wait_ge(wide_step, c + 16)
                        v.tensor_copy(agg4[:, bass.ds(t, 1), bass.ds(h, 1), :].squeeze(1).squeeze(1),
                                      duo[:, 0, 0:D1]).then_inc(wide_step, 1)
                dve.wait_ge(wide_step, 1 + W0 + NT * WT)
            dve.sem_inc(attention_done, 1)
            link(v.tensor_scalar(rden[:, :, :], agg4[:, :, :, D], 1e-37, None, ALU.max))
            v.reciprocal(rden[:, :, :], rden[:, :, :]).then_inc(rden_ready, 1)

            def x1_norm(t, s, q):
                bt = at_mid(base, t)
                dve.wait_ge(xr_in[s], q * 32 + 32)
                dve.wait_ge(res_added, t + 1)
                v.scalar_tensor_tensor(bt, bt, 0.0, xres[0][s], ALU.max, ALU.add).then_inc(x1_ready, 1)
                dve.wait_ge(x1_ready, t + 1)
                dve.wait_ge(h2_turned, t + 1)
                dve.wait_ge(h2_out[s], q * 16)
                norm(t, bt, xg[s], var2_ready, sd2_ready, h2_ready,
                     (lambda: largest(t - 3)) if t >= 3 else None)

            def largest(t):
                dve.wait_ge(logits_read, t + 1)
                v.max(mx8[:, t, :], lg[:, t, :]).then_inc(maxed, 1)
                dve.wait_ge(maxed, t + 1)
                v.max_index(ix8[:, t, :], mx8[:, t, :], lg[:, t, :]).then_inc(maxed_index, 1)

            for t in range(NT):
                x1_norm(t, t % 2, t // 2)

            dve.wait_ge(const2_ready, 1)
            for t in range(NT - 3, NT):
                largest(t)
            dve.wait_ge(maxed_index, NT)
            v.tensor_tensor(ex[:, :, :], lg[:, :, :], mx8[:, :, 0:1].broadcast_to([P, NT, NX]), ALU.subtract)\
                .then_inc(ex_lg, 1)
            v.tensor_tensor(ex1[:, :], mx8[:, :, 1], mx8[:, :, 0], ALU.subtract).then_inc(ex_in, 1)
            link(v.tensor_copy(ixf[:, :, :], ix8[:, :, 0:2]))
            for k in range(2):
                link(v.tensor_tensor(mk[:, :, k, :], iota_x[:, :].unsqueeze(1).broadcast_to([P, NT, NX]),
                                     ixf[:, :, k:k + 1].broadcast_to([P, NT, NX]), ALU.is_equal))
            link(v.tensor_scalar(mk[:, NT - 1], mk[:, NT - 1], valid[:, 0:1], None, ALU.mult))
            link(v.tensor_tensor(msum[:, :, :], mk[:, :, 0, :], mk[:, :, 1, :], ALU.add))
            link(v.memset(macc[:, 0, :], 0.0))
            for t in range(1, NT):
                link(v.tensor_tensor(macc[:, t, :], macc[:, t - 1, :], msum[:, t - 1, :], ALU.add))
            dve.sem_inc(m_ready, 1)
            dve.wait_ge(ex_ready, 1)
            link(v.tensor_reduce(pr[:, 0, :], ex[:, :, :], AX.X, ALU.add))
            link(v.reciprocal(pr[:, 0, :], pr[:, 0, :]))
            link(v.tensor_tensor(pr[:, 1, :], ex1[:, :], pr[:, 0, :], ALU.mult))
            link(v.tensor_tensor(psum_pr[:, :], pr[:, 0, :], pr[:, 1, :], ALU.add))
            link(v.tensor_scalar(psum_pr[:, :], psum_pr[:, :], 1e-20, None, ALU.add))
            link(v.reciprocal(psum_pr[:, :], psum_pr[:, :]))
            for k in range(2):
                link(v.tensor_tensor(wk[:, :, k], pr[:, k, :], psum_pr[:, :], ALU.mult))
                link(v.tensor_tensor(slb[:, :, k, 0, :], mk[:, :, k, :],
                                     pair_id[:, :].rearrange("p (t k) -> p t k", k=2)[:, :, k:k + 1]
                                     .broadcast_to([P, NT, NX]), ALU.mult))
                link(v.tensor_tensor(slb[:, :, k, 1, :], mk[:, :, k, :],
                                     wk[:, :, k:k + 1].broadcast_to([P, NT, NX]), ALU.mult))
            v.tensor_tensor(gm[:, :, :], slb[:, :, 0, 1, :], slb[:, :, 1, 1, :], ALU.add).then_inc(gm_ready, 1)
            dve.wait_ge(rank_done, 2)
            link(v.tensor_copy(n_all[:, :], banks[4][:, 0:NX]))
            link(v.tensor_copy(rk[:, :, :], banks[0][:, 0:NT * NX].rearrange("p (t n) -> p t n", t=NT)))
            for k in range(2):
                link(v.tensor_tensor(rkm[:, :, :], mk[:, :, k, :], rk[:, :, :], ALU.mult))
                link(v.tensor_reduce(rank[:, :, k], rkm[:, :, :], AX.X, ALU.add))
            v.tensor_reduce(rank_max[:, :], rank[:, :, :], AX.XY, ALU.max).then_inc(rank_max_ready, 1)
            for n in range(2 * NT):
                if n >= 4:
                    dve.wait_ge(slots_done, n - 3)
                v.tensor_scalar(sla[:, n % 4, :], iota_p[:, :], rank[:, n // 2, n % 2:n % 2 + 1], None,
                                ALU.is_equal).then_inc(sl_ready, 1)
            dve.wait_ge(slots_done, 2 * NT)
            link(v.tensor_copy(slot_v[:, :, :], banks[0][:, 0:2 * NX].rearrange("p (k n) -> p k n", k=2)))
            link(v.tensor_scalar(slot_f[:, :], slot_v[:, 0, :], 0.0, 8193.0, ALU.is_equal, ALU.mult))
            link(v.tensor_tensor(slot_f[:, :], slot_f[:, :], slot_v[:, 0, :], ALU.add))
            link(v.tensor_scalar(slot_f[:, :], slot_f[:, :], 1.0, None, ALU.subtract))
            link(v.tensor_copy(slot_s[:, :], slot_f[:, :]))
            v.tensor_single_scalar(slot_g[:, :], slot_s[:, :], 1, ALU.logical_shift_right).then_inc(slots_ready, 1)
            dve.wait_ge(rank_all_ready, 1)
            link(v.tensor_scalar(flag_f[:, 0:1], rank_all[0:1, :], float(P), None, ALU.is_ge))
            v.tensor_copy(flags[0:1, 2:3], flag_f[:, 0:1]).then_inc(flag3_ready, 1)
            def add_biases(ts):
                for t in ts:
                    dve.wait_ge(bias_done, t + 1)
                    for i in range(2):
                        v.tensor_tensor(base[:, t, i * F // 2:(i + 1) * F // 2],
                                        base[:, t, i * F // 2:(i + 1) * F // 2], bias_bank(t, i), ALU.add)\
                            .then_inc(base_ready, 1)

            add_biases(range(BIAS1))

            def turn(e, b):
                dve.wait_ge(xg_turned, e + 1)
                v.tensor_copy(xgT[b][:, 3:6, :], duo[:, 1, 0:3 * P].rearrange("p (c n) -> p c n", c=3))\
                    .then_inc(xgT_d, 1)

            def group(q, last):
                for s in range(WSLOTS):
                    e, b = q * WSLOTS + s, s % 2
                    if not (last and s == WSLOTS - 1):
                        turn(e + 1, 1 - b)
                    for m in range(HC):
                        dve.wait_ge(l3_done, e * 2 + (m + 1))
                        v.tensor_scalar(hid[2][b][:, m, :], banks[2 + m][:, 0:P], at_col(bT[:, 2, m, :], e),
                                        None, ALU.add).then_inc(z_ready, 1)
                    dve.wait_ge(l4_done, e + 1)
                    dve.wait_ge(y_out[b], q * 32 + 16 * (s // 2))
                    v.tensor_scalar(ys[b][:, F // 2:F], banks[5][:, 0:F // 2], at_col(slot_v[:, 1, :], e),
                                    None, ALU.mult).then_inc(yd_ready, 1)

            turn(0, 0)
            run(dve, NX // WSLOTS, group, first=True)
            with dve.If(dve.value_load(flags[0:1, 2:3]) > 0):
                step = [1]

                def then(ins):
                    ins.then_inc(extra_step, 1)
                    step[0] += 1
                    dve.wait_ge(extra_step, step[0])

                dve.wait_ge(extra_step, 1)
                then(v.tensor_single_scalar(ov_n, n_all[:, :], float(P - 1), ALU.add))
                then(v.tensor_copy(ov_ni, ov_n))
                then(v.tensor_single_scalar(ov_ni, ov_ni, 7, ALU.logical_shift_right))
                then(v.tensor_copy(ov_n, ov_ni))
                then(v.tensor_scalar(ov_n, ov_n, 1.0, 0.0, ALU.subtract, ALU.max))
                then(v.tensor_copy(ov_end[:, 0:1], ov_n[:, 0:1]))
                for i in range(1, NX):
                    then(v.tensor_tensor(ov_end[:, i:i + 1], ov_end[:, i - 1:i], ov_n[:, i:i + 1], ALU.add))
                then(v.tensor_tensor(ov_first, ov_end, ov_n, ALU.subtract))
                both = [P, OT, NX]
                then(v.tensor_tensor(ov_tab, iota_o.unsqueeze(2).broadcast_to(both),
                                     ov_first.unsqueeze(1).broadcast_to(both), ALU.is_ge))
                then(v.tensor_tensor(ov_tab2, iota_o.unsqueeze(2).broadcast_to(both),
                                     ov_end.unsqueeze(1).broadcast_to(both), ALU.is_lt))
                then(v.tensor_tensor(ov_tab, ov_tab, ov_tab2, ALU.mult))
                then(v.tensor_tensor(ov_tab, ov_tab, iota_x[:, :].unsqueeze(1).broadcast_to(both), ALU.mult))
                then(v.tensor_reduce(ov_ex, ov_tab, AX.X, ALU.add))
                then(v.tensor_copy(ov_exi, ov_ex))
                for k in range(2):
                    then(v.tensor_tensor(ov_m, mk[:, :, k, :],
                                         ov_first.unsqueeze(1).broadcast_to([P, NT, NX]), ALU.mult))
                    then(v.tensor_reduce(ov_base[:, :, k], ov_m, AX.X, ALU.add))
                then(v.tensor_copy(ov_rank_i, rank[:, :, :]))
                then(v.tensor_single_scalar(ov_hi_i, ov_rank_i, 7, ALU.logical_shift_right))
                then(v.tensor_single_scalar(ov_lo_i, ov_rank_i, P - 1, ALU.bitwise_and))
                then(v.tensor_copy(ov_hi, ov_hi_i))
                then(v.tensor_copy(ov_lo, ov_lo_i))
                then(v.tensor_scalar(ov_ge, ov_hi, 1.0, None, ALU.is_ge))
                then(v.tensor_tensor(ov_hi, ov_hi, ov_base, ALU.add))
                then(v.tensor_tensor(ov_hi, ov_hi, ov_ge, ALU.mult))
                then(v.tensor_scalar(ov_hi, ov_hi, 1.0, None, ALU.subtract))
                for i in range(2 * NT):
                    t, k = i // 2, i % 2
                    then(v.tensor_scalar(ov_a, iota_p[:, :], ov_lo[:, t, k:k + 1], None, ALU.is_equal))
                    then(v.tensor_scalar(ov_b[:, 0, :], iota_o, ov_hi[:, t, k:k + 1], pair_id[:, i:i + 1],
                                         ALU.is_equal, ALU.mult))
                    v.tensor_scalar(ov_b[:, 1, :], iota_o, ov_hi[:, t, k:k + 1], wk[:, t, k:k + 1],
                                    ALU.is_equal, ALU.mult).then_inc(extra_step, 1)
                    step[0] += 2
                    dve.wait_ge(extra_step, step[0])
                then(v.tensor_copy(ov_v, banks[0][:, 0:2 * OT].rearrange("p (k n) -> p k n", k=2)))
                then(v.tensor_scalar(ov_f, ov_v[:, 0, :], 0.0, FAR + 1.0, ALU.is_equal, ALU.mult))
                then(v.tensor_tensor(ov_f, ov_f, ov_v[:, 0, :], ALU.add))
                then(v.tensor_scalar(ov_f, ov_f, 1.0, None, ALU.subtract))
                then(v.tensor_copy(ov_s, ov_f))
                then(v.tensor_single_scalar(ov_g, ov_s, 1, ALU.logical_shift_right))
                assert step[0] == X0 + 1, step[0]
                with dve.Fori(0, OT) as j:
                    n = j * XK + (X0 + 1)
                    e = dve.value_load(at_col(ov_exi[0:1, :], j), min_val=0, max_val=NX - 1)
                    dve.wait_ge(extra_step, n + 3)
                    for i in range(2):
                        v.tensor_copy(xgT[0][:, 3 * i:3 * i + 3, :],
                                      duo[:, i, 0:3 * P].rearrange("p (c n) -> p c n", c=3))\
                            .then_inc(extra_step, 1)
                    dve.wait_ge(extra_step, n + 13)
                    for m in range(HC):
                        v.tensor_scalar(hid[2][0][:, m, :], banks[2 + m][:, 0:P], at_col(bT[:, 2, m, :], e),
                                        None, ALU.add).then_inc(extra_step, 1)
                    dve.wait_ge(extra_step, n + 16)
                    for i in range(2):
                        v.tensor_scalar(ys[0][:, i * F // 2:(i + 1) * F // 2], banks[4 + i][:, 0:F // 2],
                                        at_col(ov_v[:, 1, :], j), None, ALU.mult).then_inc(extra_step, 1)
                dve.wait_ge(extra_step, X0 + OT * XK + 1)

            add_biases(range(BIAS1, NT))
            dve.wait_ge(base_ready, 2 * NT)
            for t in range(NT):
                dve.wait_ge(ypair_in[t % YR], 16 * (t // YR + 1))
                for k in range(2):
                    ins = v.tensor_tensor(base[0:rows(t), t, :], base[0:rows(t), t, :],
                                          ypair[t % YR][0:rows(t), F * k:F * (k + 1)], ALU.add)
                    if k == 0:
                        link(ins)
                    else:
                        ins.then_inc(sum_ready, 1)

        @block.scalar
        def _(act):
            a = nc.scalar
            act.sem_inc(signed, 2 * NS)

            def deviation(t, var_ready, sd_ready):
                act.wait_ge(var_ready, t + 1)
                a.activation(sd[:, :], ve[:, :], ACT.Sqrt).then_inc(sd_ready, 1)

            def one_hot_rows(q, part):
                k = q * 2 + part
                n = CRING // 2
                act.wait_ge(window_done, q * WSTEP + (part + 1) * (WSTEP // 2))
                if not (isinstance(k, int) and k == 0):
                    act.wait_ge(oha_ready, k * n)
                for r in range(n):
                    a.activation(apart[:, part, r, :], iota_p[:, :], ACT.Abs,
                                 bias=at_col(jneg, q * CRING + part * n + r)).then_inc(apart_ready, 1)
                act.wait_ge(apart_ready, k * n + n)
                a.activation(oha[:, part * n:(part + 1) * n, :], apart[:, part], ACT.Relu, scale=-1.0,
                             bias=ones_f[:, 0:1]).then_inc(oha_ready, n)

            act.wait_ge(const_ready, 1)
            act.wait_ge(jneg_ready, 1)
            one_hot_rows(0, 0)
            deviation(0, var1_ready, sd1_ready)

            def tiles1(q, last):
                for s in range(2):
                    t = q * 2 + s
                    one_hot_rows(t * 2, 1)
                    act.wait_ge(h_turned, t + 3)
                    for i in range(2):
                        a.activation(hTt[s][:, 3 * i:3 * i + 3, :],
                                     duo[:, i, 0:3 * P].rearrange("p (c n) -> p c n", c=3), ACT.Copy)\
                            .then_inc(hT_ready, 1)
                    one_hot_rows(t * 2 + 1, 0)
                    if not (last and s == 1):
                        deviation(t + 1, var1_ready, sd1_ready)
                    one_hot_rows(t * 2 + 1, 1)
                    act.wait_ge(ft_done, t * 2 + 1)
                    a.activation(at_mid(ft4, t)[:, 0:8, 0:D], banks[2][:, :].rearrange("p (h e) -> p h e", e=D),
                                 ACT.Copy).then_inc(ft_ready, 1)
                    a.activation(at_mid(ft4, t)[:, 8:H, 0:D],
                                 banks[3][:, 0:4 * D].rearrange("p (h e) -> p h e", e=D), ACT.Copy)\
                        .then_inc(ft_ready, 1)
                    if not (last and s == 1):
                        one_hot_rows(t * 2 + 2, 0)

            run(act, NT // 2, tiles1)
            act.wait_ge(fa_ready, 1)
            for b in range(2):
                a.activation(e12[:, b], a12[:, :, 0:H], ACT.Exp, bias=nA[:, b:b + 1],
                             scale=1.0 if b == 0 else SLOPE).then_inc(e_made, 1)
            a.activation(f12[:, :, :, :].rearrange("p b t h -> p (b t h)"),
                         fa[:, :, :, :].rearrange("p b t h -> p (b t h)"), ACT.Exp).then_inc(e_made, 1)
            act.wait_ge(e_made, 3)
            act.sem_inc(e_ready, 1)
            act.wait_ge(a2_turned, 1)
            for i in range(3):
                n = min(512, NP - 512 * i)
                a.activation(a2T[:, 512 * i:512 * i + n], banks[i][0:H, 0:n], ACT.Copy).then_inc(a2T_ready, 1)
            act.wait_ge(a2T_ready, 3)

            def pick(h):
                act.wait_ge(a2_spread, h)
                a.activation(a2m[:, :], a2T[:, :], ACT.Copy, scale=at_col(ident[0:H, :], h)).then_inc(a2m_ready, 1)

            def spread0(h):
                act.wait_ge(a2_spread, h + 1)
                act.wait_ge(compared, h * (2 * SIGN0) + SIGN0)
                act.wait_ge(signed, h * (2 * NS) + NS)
                a.activation(a2b[:, 0:512], banks[4][:, :], ACT.Copy).then_inc(a2b_ready, 1)
                a.activation(a2b[:, 512:PART], duo[:, 0, 0:PART - 512], ACT.Copy).then_inc(a2b_ready, 1)

            def spread1(h):
                act.wait_ge(compared, h * (2 * SIGN0) + 2 * SIGN0)
                act.wait_ge(signed, h * (2 * NS) + 2 * NS)
                a.activation(a2b[:, PART:1024], duo[:, 0, PART - 512:512], ACT.Copy).then_inc(a2b_ready, 1)
                a.activation(a2b[:, 1024:NP], duo[:, 1, 0:NP - 1024], ACT.Copy).then_inc(a2b_ready, 1)

            def high(h, s):
                act.wait_ge(x_made, h * 2 + 2)
                act.wait_ge(sums_done, h * NT)
                a.activation(xp[s][:, :, 0], x12, ACT.Copy).then_inc(hi_ready, 1)

            def middle(h, s):
                act.wait_ge(rest_made, h + 1)
                a.activation(xp[s][:, :, 1], x12, ACT.Copy).then_inc(mid_ready, 1)

            def second_sums(h, s, ts):
                for t in ts:
                    r = (s * NT + t) % SRING
                    act.wait_ge(sums_done, h * NT + (t + 1 + NT))
                    a.activation(t2[:, r, :], banks[r][:, D1:2 * D1], ACT.Copy,
                                 scale=at_col(f12[:, 1, t, :], h)).then_inc(t2_ready, 1)

            def signs(h, i, jts):
                lo, hi = ITS[i]
                for jt in jts:
                    a.activation(mask[i][:, jt, :], a2b[:, lo * P:hi * P], ACT.Sign,
                                 bias=at_col(a12[:, jt, 0:H], h)).then_inc(signed, 1)

            def part(h, s, i, sign_h, sign_i, work):
                t = i * (NT // 2)
                if sign_h is not None:
                    act.wait_ge(a2b_ready, sign_h * 4 + (2 if sign_i == 0 else 4))
                    act.wait_ge(sums_done, sign_h * NT + (ITS[0][1] if sign_i == 0 else NT))
                    act.sem_inc(signs_begun, 1)
                    signs(sign_h, sign_i, range(SIGN0, NT))
                for k in range(NT // 2):
                    second_sums(h, s, (t + k,))
                    if k in work:
                        work[k]()

            def heads(hh, last):
                for s in range(2):
                    h = hh * 2 + s
                    more = not (last and s == 1)
                    part(h, s, 0, h, 1, {0: lambda: high(h + 1, 1 - s), 2: lambda: spread0(h + 1)} if more else {})
                    work = {0: lambda: middle(h + 1, 1 - s), 2: lambda: spread1(h + 1)}
                    if not last:
                        work[3] = lambda: pick(h + 2)
                    if more:
                        part(h, s, 1, h + 1, 0, work)
                    else:
                        part(h, s, 1, None, None, {})

            pick(0)
            act.wait_ge(counts_added, 1)
            for jt in range(ACAST):
                a.activation(cbf[:, jt, :], c32[:, jt, 0:NP], ACT.Copy, accum_out=degree[:, jt:jt + 1])\
                    .then_inc(counts_ready, 1)
                if jt == 1:
                    high(0, 0)
                elif jt == 3:
                    middle(0, 0)
            spread0(0)
            spread1(0)
            act.wait_ge(flag2_ready, 1)
            with act.If(act.value_load(flags[0:1, 1:2]) < 1):
                act.wait_ge(a2b_ready, 4)
                act.wait_ge(neg_ready, 2)
                signs(0, 0, range(SIGN0, NT))
                pick(1)
                run(act, H // 2, heads)
            with act.Else():
                act.wait_ge(wide_step, 2)
                for i in range(3):
                    n = min(512, NP - 512 * i)
                    a.activation(a2T[:, 512 * i:512 * i + n], banks[i][0:H, 0:n], ACT.Copy).then_inc(wide_step, 1)
                with act.Fori(0, NT) as t:
                    with act.Fori(0, H) as h:
                        c = t * WT + h * WH + (W0 + 7)
                        act.wait_ge(wide_step, c)
                        a.activation(a2m[:, :], a2T[:, :], ACT.Copy, scale=at_col(ident[0:H, :], h))\
                            .then_inc(wide_step, 1)
                        act.wait_ge(wide_step, c + 9)
                        a.activation(e_row, e_row, ACT.Exp).then_inc(wide_step, 1)

            deviation(0, var2_ready, sd2_ready)

            def logits(t, s):
                act.wait_ge(logits_done, t + 1)
                a.activation(at_mid(lg, t), banks[4 + s][:, 0:NX], ACT.Copy).then_inc(logits_read, 1)

            def tiles2(q, last):
                for s in range(2):
                    t = q * 2 + s
                    if not (last and s == 1):
                        deviation(t + 1, var2_ready, sd2_ready)
                    act.wait_ge(h2_turned, t + 3)
                    for i in range(2):
                        a.activation(xgT[s][:, 3 * i:3 * i + 3, :],
                                     turned2(s, i).rearrange("p (c n) -> p c n", c=3), ACT.Copy)\
                            .then_inc(h2T_ready, 1)
                    if not (isinstance(t, int) and t == 0):
                        logits(t - 1, 1 - s)

            run(act, NT // 2, tiles2, first=True)
            logits(NT - 1, 1)
            act.wait_ge(ex_in, 1)
            act.wait_ge(ex_lg, 1)
            a.activation(ex[:, :, :], ex[:, :, :], ACT.Exp).then_inc(ex_made, 1)
            a.activation(ex1[:, :], ex1[:, :], ACT.Exp).then_inc(ex_made, 1)
            act.wait_ge(ex_made, 2)
            act.sem_inc(ex_ready, 1)
            act.wait_ge(gm_turned, 1)
            for i in range(3):
                n = min(512, NP - 512 * i)
                a.activation(gmT[:, 512 * i:512 * i + n], banks[1 + i][0:NX, 0:n], ACT.Copy).then_inc(gmT_ready, 1)

            def turn(e, b):
                act.wait_ge(xg_turned, e + 1)
                a.activation(xgT[b][:, 0:3, :], duo[:, 0, 0:3 * P].rearrange("p (c n) -> p c n", c=3), ACT.Copy)\
                    .then_inc(xgT_a, 1)

            def gelu1(e, b):
                for m in range(HC):
                    act.wait_ge(l1_done, e * 2 + (m + 1))
                    a.activation(hid[0][b][:, m, :], banks[m][:, 0:P], ACT.Gelu,
                                 bias=at_col(bT[:, 0, m, :], e)).then_inc(g1_ready, 1)

            def group(q, last):
                for s in range(WSLOTS):
                    e, b = q * WSLOTS + s, s % 2
                    more = not (last and s == WSLOTS - 1)
                    if more:
                        turn(e + 1, 1 - b)
                    for m in range(HC):
                        act.wait_ge(l2_done, e * 2 + (m + 1))
                        a.activation(hid[1][b][:, m, :], banks[2 + m][:, 0:P], ACT.Gelu,
                                     bias=at_col(bT[:, 1, m, :], e)).then_inc(g2_ready, 1)
                    if more:
                        gelu1(e + 1, 1 - b)
                    act.wait_ge(l4a_done, e + 1)
                    act.wait_ge(y_out[b], q * 32 + 16 * (s // 2))
                    a.activation(ys[b][:, 0:F // 2], banks[4][:, 0:F // 2], ACT.Copy,
                                 scale=at_col(slot_v[:, 1, :], e)).then_inc(ya_ready, 1)

            turn(0, 0)
            gelu1(0, 0)
            run(act, NX // WSLOTS, group, first=True)
            act.wait_ge(flag3_ready, 1)
            with act.If(act.value_load(flags[0:1, 2:3]) > 0):
                with act.Fori(0, OT) as j:
                    n = j * XK + (X0 + 1)
                    act.wait_ge(extra_step, n)
                    e = act.value_load(at_col(ov_exi[0:1, :], j), min_val=0, max_val=NX - 1)
                    for k in range(2):
                        act.wait_ge(extra_step, n + (6 if k == 0 else 9))
                        for m in range(HC):
                            a.activation(hid[k][0][:, m, :], banks[2 * k + m][:, 0:P], ACT.Gelu,
                                         bias=at_col(bT[:, k, m, :], e)).then_inc(extra_step, 1)

        @block.tensor
        def _(pe):
            T = nc.tensor
            pe.sem_inc(window_done, WSTEP)
            pe.sem_inc(h_turned, 2)
            pe.sem_inc(h2_turned, 2)
            pe.sem_inc(sums_done, NT)
            pe.wait_ge(const_ready, 1)

            pe.wait_ge(edges_float, 4)
            for k in range(2):
                T.transpose(banks[0][:, k * ETP:k * ETP + P], edges_f[:, k, :], ident[:, :])
                T.transpose(banks[0][:, k * ETP + P:(k + 1) * ETP], edges_f[0:ET1, 2 + k, :], ident[0:ET1, 0:ET1])
            T.transpose(banks[1][0:1, 0:P], tmin[:, 0:1], ident[:, :])
            T.transpose(banks[1][0:1, P:ETP], tmin[0:ET1, 1:2], ident[0:ET1, 0:ET1]).then_inc(edges_turned, 1)
            pe.wait_ge(lo_ready, 1)
            T.matmul(banks[2][:, 0:NG], ones_f[0:1, :], lo_min[0:1, :], start=True, stop=True).then_inc(lo_spread, 1)
            pe.wait_ge(gnnw_in, 16 * (4 + 4))
            for k in range(2):
                ins = T.transpose(banks[3][:, k * P:(k + 1) * P], bdn[:, k, :], ident[:, :])
            ins.then_inc(bd_turned, 1)
            T.matmul(banks[4][:, 0:C6 * 2 * H], bdn[:, 0, :], at[:, :, :].rearrange("p c n -> p (c n)"),
                     start=True, stop=True).then_inc(bda_done, 1)
            pe.wait_ge(key_ready, 1)
            pe.wait_ge(bd_ready, 1)

            def windows(q, part):
                for w in range(part * WSTEP // 2, (part + 1) * WSTEP // 2):
                    pe.wait_ge(window_added, q * WSTEP + (w + 1))
                    for k in range(GSIZE):
                        r = w * GSIZE + k
                        pe.wait_ge(oha_ready, q * CRING + (r + 1))
                        pe.wait_ge(ohb_ready, q * CRING + (r + 1))
                        ins = T.matmul(banks[w % WRING][:, 0:KW], oha[:, r, :], ohb[:, r, :],
                                       start=(k == 0), stop=(k == GSIZE - 1))
                    ins.then_inc(window_done, 1)

            pe.wait_ge(bda_ready, 1)

            def transposes(tile, done):
                for c in range(C6):
                    ins = T.transpose(duo[:, c // 3, P * (c % 3):P * (c % 3) + P],
                                      tile(c), ident[:, :])
                ins.then_inc(done, 1)

            def tiles1(q, last):
                for s in range(2):
                    t = q * 2 + s
                    windows(t * 2, 0)
                    pe.wait_ge(h_ready, t + 1)
                    pe.wait_ge(hT_ready, t * 2)
                    transposes(lambda c: ht[s][:, c * P:(c + 1) * P], h_turned)
                    windows(t * 2, 1)
                    pe.wait_ge(hT_ready, t * 2 + 2)
                    pe.wait_ge(ft_ready, t * 2)
                    for c in range(C6):
                        ins = T.matmul(banks[2 + c // 4][:, P * (c % 4):P * (c % 4) + P], hTt[s][:, c, :],
                                       bd[:, 0, :], start=True, stop=True)
                    ins.then_inc(ft_done, 1)
                    windows(t * 2 + 1, 0)
                    pe.wait_ge(res_copied, t * 3)
                    for c in range(C6):
                        T.matmul(banks[4 + c // 4][:, P * (c % 4):P * (c % 4) + P], hTt[s][:, c, :],
                                 bd[:, 1, :], start=True, stop=True)
                    windows(t * 2 + 1, 1)
                    for c in range(C6):
                        ins = T.matmul(banks[5][:, 256:256 + 2 * H], hTt[s][:, c, :], bda[:, c, :],
                                       start=(c == 0), stop=(c == C6 - 1))
                    ins.then_inc(ft_done, 1)

            run(pe, NT // 2, tiles1, first=True)
            pe.wait_ge(flag1_ready, 1)
            with pe.If(pe.value_load(flags[0:1, 0:1]) > 0):
                pe.sem_inc(more_step, 1)
                with pe.Fori(0, MORE) as p_:
                    with pe.Fori(0, NG) as gq:
                        pe.wait_ge(more_step, p_ * MK + gq * 5 + 12)
                        for k in range(GSIZE):
                            ins = T.matmul(banks[0][:, 0:KW], oha[:, k, :], ohb[:, k, :],
                                           start=(k == 0), stop=(k == GSIZE - 1))
                        ins.then_inc(more_step, 1)
                pe.wait_ge(more_step, 1 + MORE * MK)
            pe.wait_ge(window_added, WRING + NG)
            pe.wait_ge(res_copied, NT * 3)
            pe.wait_ge(ft_ready, NT * 2)
            for t in range(NT):
                ins = T.transpose(banks[t // 4][0:H, P * (t % 4):P * (t % 4) + P], a12[:, t, H:2 * H], ident[:, :])
            ins.then_inc(a2_turned, 1)
            pe.wait_ge(small_in, 16 * 5)
            for c in range(C6):
                T.transpose(banks[3][:, c * NX:(c + 1) * NX], chunks(gate_n[:, :], c), ident[0:NX, 0:NX])
            for k in range(3):
                for c in range(HC):
                    n = (C6 + k * HC + c) * NX
                    ins = T.transpose(banks[3][:, n:n + NX], chunks(bn[:, k, :], c), ident[0:NX, 0:NX])
            ins.then_inc(small_turned, 1)

            def spread(h):
                pe.wait_ge(a2m_ready, h + 1)
                pe.wait_ge(a2b_ready, h * 4)
                T.matmul(banks[4][:, :], ones_f[0:H, :], a2m[:, 0:512], start=True, stop=True)
                T.matmul(duo[:, 0, :], ones_f[0:H, :], a2m[:, 512:1024], start=True, stop=True)
                T.matmul(duo[:, 1, 0:NP - 1024], ones_f[0:H, :], a2m[:, 1024:NP], start=True, stop=True)\
                    .then_inc(a2_spread, 1)

            def heads(hh, last):
                for s in range(2):
                    h = hh * 2 + s
                    if not (last and s == 1):
                        spread(h + 1)
                    pe.wait_ge(xp_ready, h + 2)
                    for i, (lo, hi) in enumerate(ITS):
                        pe.wait_ge(mask_ready, h * 2 + (i + 1))
                        for t in range(lo, hi):
                            r = (s * NT + t) % SRING
                            pe.wait_ge(sums_added, h * NT + (t + 1))
                            cols = slice((t - lo) * P, (t - lo + 1) * P)
                            for jt in range(NT):
                                both = 2 if jt < NEG else 1
                                for k in range(3):
                                    T.matmul(banks[r][:, 0:both * D1], mask[i][:, jt, cols],
                                             xp[s][:, jt, k, 0:both].rearrange("p b e -> p (b e)"),
                                             start=(jt == 0 and k == 0), stop=False)
                            for jt in range(NT):
                                for k in range(3):
                                    ins = T.matmul(banks[r][:, D1:2 * D1], nmask[i][:, jt, cols],
                                                   xp[s][:, jt, k, 1, :], start=False,
                                                   stop=(jt == NT - 1 and k == 2))
                            ins.then_inc(sums_done, 1)

            pe.wait_ge(a2T_ready, 3)
            pe.wait_ge(smallT_ready, 2)
            spread(0)
            pe.wait_ge(const2_ready, 1)
            pe.wait_ge(flag2_ready, 1)
            with pe.If(pe.value_load(flags[0:1, 1:2]) < 1):
                pe.wait_ge(neg_ready, 2)
                run(pe, H // 2, heads)
            with pe.Else():
                pe.sem_inc(wide_step, 1)
                for t in range(NT):
                    ins = T.transpose(banks[t // 4][0:H, P * (t % 4):P * (t % 4) + P], a12[:, t, 0:H], ident[:, :])
                ins.then_inc(wide_step, 1)
                with pe.Fori(0, NT) as t:
                    n = t * WT + W0
                    pe.wait_ge(wide_step, n + 2)
                    for jt in range(NT):
                        ins = T.transpose(banks[jt // 4][:, P * (jt % 4):P * (jt % 4) + P], c_in[:, jt, :],
                                          ident[:, :])
                    ins.then_inc(wide_step, 1)
                    with pe.Fori(0, H) as h:
                        c = n + h * WH + 7
                        pe.wait_ge(wide_step, c + 1)
                        for i in range(3):
                            m = min(512, NP - 512 * i)
                            ins = T.matmul(banks[3 + i][:, 0:m], ones_f[0:H, :], a2m[:, 512 * i:512 * i + m],
                                           start=True, stop=True)
                        ins.then_inc(wide_step, 1)
                        pe.wait_ge(wide_step, c + 11)
                        for jt in range(NT):
                            ins = T.transpose(banks[jt // 4][:, P * (jt % 4):P * (jt % 4) + P],
                                              p_row[:, jt * P:(jt + 1) * P], ident[:, :])
                        ins.then_inc(wide_step, 1)
                        pe.wait_ge(wide_step, c + 15)
                        for jt in range(NT):
                            ins = T.matmul(duo[:, 0, 0:D1], p_t[:, jt, :], at_mid(ft4[:, jt], h),
                                           start=(jt == 0), stop=(jt == NT - 1))
                        ins.then_inc(wide_step, 1)

            def turn2(t, s):
                pe.wait_ge(h2_ready, t + 1)
                if not (isinstance(t, int) and t < 2):
                    pe.wait_ge(h2T_ready, t * 2 - 2)
                for c in range(C6):
                    ins = T.transpose(turned2(s, c // 3)[:, P * (c % 3):P * (c % 3) + P], chunks(xg[s], c),
                                      ident[:, :])
                ins.then_inc(h2_turned, 1)

            def tiles2(q, last):
                for s in range(2):
                    t = q * 2 + s
                    if not (last and s == 1):
                        turn2(t + 1, 1 - s)
                    pe.wait_ge(h2T_ready, t * 2 + 2)
                    if not (isinstance(t, int) and t < 2):
                        pe.wait_ge(logits_read, t - 1)
                    for c in range(C6):
                        ins = T.matmul(banks[4 + s][:, 0:NX], xgT[s][:, c, :], gateT[:, c, :],
                                       start=(c == 0), stop=(c == C6 - 1))
                    ins.then_inc(logits_done, 1)

            turn2(0, 0)
            run(pe, NT // 2, tiles2, first=True)
            pe.wait_ge(m_ready, 1)
            T.matmul(banks[0][:, 0:NT * NX], before[:, :], msum[:, :, :].rearrange("p t n -> p (t n)"),
                     start=True, stop=False)
            T.matmul(banks[0][:, 0:NT * NX], ones_b[:, :], macc[:, :, :].rearrange("p t n -> p (t n)"),
                     start=False, stop=True).then_inc(rank_done, 1)
            for k, chosen in enumerate((macc, msum)):
                ins = T.matmul(banks[4][:, 0:NX], ones_b[:, :], chosen[:, NT - 1, :], start=(k == 0), stop=(k == 1))
            ins.then_inc(rank_done, 1)
            pe.wait_ge(gm_ready, 1)
            for t in range(NT):
                ins = T.transpose(banks[1 + t // 4][0:NX, P * (t % 4):P * (t % 4) + P], gm[:, t, :], ident[:, :])
            ins.then_inc(gm_turned, 1)
            for n in range(2 * NT):
                pe.wait_ge(sl_ready, n + 1)
                T.matmul(banks[0][:, 0:2 * NX], sla[:, n % 4, :],
                         slb[:, n // 2, n % 2].rearrange("p k n -> p (k n)"),
                         start=(n == 0), stop=(n == 2 * NT - 1)).then_inc(slots_done, 1)
            pe.wait_ge(gmT_ready, 3)
            pe.wait_ge(slots_ready, 1)

            def biases(ts):
                for t in ts:
                    if t >= 3:
                        pe.wait_ge(base_ready, 2 * (t - 2))
                    for i in range(2):
                        ins = T.matmul(bias_bank(t, i), gmT[:, t * P:(t + 1) * P],
                                       bln[:, i * F // 2:(i + 1) * F // 2], start=True, stop=True)
                    ins.then_inc(bias_done, 1)

            biases(range(BIAS1))
            pe.wait_ge(base_ready, 2 * BIAS1)

            def turn(e, q, s):
                pe.wait_ge(xg_in[s], q * 16 + 16)
                pe.wait_ge(xgT_a, e)
                pe.wait_ge(xgT_d, e)
                transposes(lambda c: chunks(xg[s], c), xg_turned)

            def layer1(e, s, b, m, q):
                if m == 0:
                    pe.wait_ge(w_in[s], q * 64 + 64)
                    pe.wait_ge(xgT_a, e + 1)
                    pe.wait_ge(xgT_d, e + 1)
                pe.wait_ge(g1_ready, e * 2 + (m - 1) if not isinstance(e, int) or e > 0 else 0)
                for c in range(C6):
                    ins = T.matmul(banks[m][:, 0:P], chunks(w1s[s][:, c, :], m), xgT[b][:, c, :],
                                   start=(c == 0), stop=(c == C6 - 1))
                ins.then_inc(l1_done, 1)

            def layer(w, xin, done):
                for m in range(HC):
                    for c in range(HC):
                        ins = T.matmul(banks[2 + m][:, 0:P], chunks(w[:, c, :], m), xin[:, c, :],
                                       start=(c == 0), stop=(c == HC - 1))
                    ins.then_inc(done, 1)

            def group(q, last):
                for s in range(WSLOTS):
                    e, b = q * WSLOTS + s, s % 2
                    more = not (last and s == WSLOTS - 1)
                    q1, s1 = (q, s + 1) if s < WSLOTS - 1 else (q + 1, 0)
                    if more:
                        turn(e + 1, q1, s1)
                    pe.wait_ge(g1_ready, e * 2 + 2)
                    pe.wait_ge(z_ready, e * 2)
                    layer(w2s[s], hid[0][b], l2_done)
                    if more:
                        layer1(e + 1, s1, 1 - b, 0, q1)
                    pe.wait_ge(g2_ready, e * 2 + 2)
                    layer(w3s[s], hid[1][b], l3_done)
                    if more:
                        layer1(e + 1, s1, 1 - b, 1, q1)
                    pe.wait_ge(z_ready, e * 2 + 2)
                    pe.wait_ge(ya_ready, e)
                    pe.wait_ge(yd_ready, e)
                    for i, done in enumerate((l4a_done, l4_done)):
                        for c in range(HC):
                            ins = T.matmul(banks[4 + i][:, 0:F // 2], hid[2][b][:, c, :],
                                           wls[s][:, c, i * F // 2:(i + 1) * F // 2],
                                           start=(c == 0), stop=(c == HC - 1))
                        ins.then_inc(done, 1)

            turn(0, 0, 0)
            for m in range(HC):
                layer1(0, 0, 0, m, 0)
            run(pe, NX // WSLOTS, group, first=True)
            pe.wait_ge(flag3_ready, 1)
            with pe.If(pe.value_load(flags[0:1, 2:3]) > 0):
                for i in range(2 * NT):
                    pe.wait_ge(extra_step, XS + 4 * i + 3)
                    T.matmul(banks[0][:, 0:2 * OT], ov_a, ov_b.rearrange("p k n -> p (k n)"),
                             start=(i == 0), stop=(i == 2 * NT - 1)).then_inc(extra_step, 1)
                with pe.Fori(0, OT) as j:
                    n = j * XK + (X0 + 1)
                    pe.wait_ge(extra_step, n + 2)
                    pe.wait_ge(ex_in_x, j * 16 + 16)
                    transposes(lambda c: chunks(xg[0], c), extra_step)
                    pe.wait_ge(extra_step, n + 5)
                    pe.wait_ge(ex_in_w, j * 64 + 64)
                    for m in range(HC):
                        for c in range(C6):
                            ins = T.matmul(banks[m][:, 0:P], chunks(w1s[0][:, c, :], m), xgT[0][:, c, :],
                                           start=(c == 0), stop=(c == C6 - 1))
                    ins.then_inc(extra_step, 1)
                    for k, w in enumerate((w2s[0], w3s[0])):
                        pe.wait_ge(extra_step, n + (8 if k == 0 else 11))
                        for m in range(HC):
                            for c in range(HC):
                                ins = T.matmul(banks[2 + m][:, 0:P], chunks(w[:, c, :], m), hid[k][0][:, c, :],
                                               start=(c == 0), stop=(c == HC - 1))
                        ins.then_inc(extra_step, 1 if k == 0 else 2)
                    pe.wait_ge(extra_step, n + 15)
                    for i in range(2):
                        for c in range(HC):
                            ins = T.matmul(banks[4 + i][:, 0:F // 2], hid[2][0][:, c, :],
                                           wls[0][:, c, i * F // 2:(i + 1) * F // 2],
                                           start=(c == 0), stop=(c == HC - 1))
                    ins.then_inc(extra_step, 1)
                pe.wait_ge(extra_step, X0 + OT * XK + 1)
            pe.wait_ge(z_ready, 2 * NX)
            pe.wait_ge(ya_ready, NX)
            pe.wait_ge(yd_ready, NX)
            biases(range(BIAS1, NT))


_INS = ['x', 'src', 'dst', 'L0_gnn_W_fc', 'L0_gnn_attn_l', 'L0_gnn_attn_r', 'L0_gnn_W_res', 'L0_ffn_gate_w',
        'L0_ffn_W1', 'L0_ffn_b1', 'L0_ffn_W2', 'L0_ffn_b2', 'L0_ffn_W3', 'L0_ffn_b3', 'L0_ffn_Wl', 'L0_ffn_bl']


def kernel(**inputs):
    import numpy as _np
    import concourse.bacc as _bacc
    from concourse import mybir as _mybir
    from concourse.bass_utils import run_bass_kernel_spmd as _run

    nc = _bacc.Bacc("TRN2", target_bir_lowering=False, num_devices=1)
    arrays, args = {}, []
    for name in _INS:
        a = _np.ascontiguousarray(inputs[name])
        arrays[f"in_{name}"] = a
        args.append(nc.dram_tensor(f"in_{name}", a.shape, _mybir.dt.from_np(a.dtype), kind="ExternalInput").ap())
    n, f = inputs['x'].shape
    padded = -(-n // 128) * 128
    out = nc.dram_tensor("out", (n, f), _mybir.dt.float32, kind="ExternalOutput").ap()
    h2 = nc.dram_tensor("h2", (padded, f), _mybir.dt.float32, kind="Internal").ap()
    y = nc.dram_tensor("y", (2 * padded, f), _mybir.dt.float32, kind="Internal").ap()
    res = nc.dram_tensor("res", (padded, f), _mybir.dt.float32, kind="Internal").ap()
    gnn_moe_kernel(nc, *args, out, h2, y, res)
    r = _run(nc, [arrays], core_ids=[0])
    return r.results[0]["out"]
```
